# Optimizing a Trainium2 kernel written in Bass

```python
import numpy as np
import jax
import jax.numpy as jnp

def _softmax(x, axis=-1):
    return jax.nn.softmax(x, axis=axis)

def _gelu(x):
    return jax.nn.gelu(x, approximate=True)

def _silu(x):
    return jax.nn.silu(x)

def _sigmoid(x):
    return jax.nn.sigmoid(x)

def _layernorm(x, axis=-1, eps=1e-05):
    m = jnp.mean(x, axis=axis, keepdims=True)
    v = jnp.var(x, axis=axis, keepdims=True)
    return (x - m) / jnp.sqrt(v + eps)

def _scatter_add(tgt, idx, src, axis=0):
    return tgt.at[idx].add(src)

def _segment_sum(src, seg, n):
    return jax.ops.segment_sum(src, seg, n)
kernel_name = 'mk_gnn_resnorm_d4_gnn_r8_f91b60'

def setup_inputs(seed: int=0):
    np.random.seed(seed)
    _w = jnp.asarray

    def _rec_inputs():
        import jax
        import jax.numpy as jnp
        _gk = jax.random.key(seed)
        x = -8.776e-05 + 1 * jax.random.normal(jax.random.fold_in(_gk, 1), (6250, 256), jnp.float32)
        src = jax.random.randint(jax.random.fold_in(_gk, 2), (100000,), 0, 6250, jnp.int32)
        dst = jnp.minimum((6250 * jax.random.uniform(jax.random.fold_in(_gk, 3), (100000,)) ** 2.0).astype(jnp.int32), 49999)
        _o = jnp.argsort(dst, stable=True)
        src = src[_o]
        dst = dst[_o]
        edge_attr_10 = jax.random.uniform(jax.random.fold_in(_gk, 13), (100000, 10), jnp.float32, 0.0, 1)
        edge_attr_256 = -6.47781e-05 + 0.999943 * jax.random.normal(jax.random.fold_in(_gk, 14), (100000, 256), jnp.float32)
        edge_attr_4 = 0.000924777 + 0.999162 * jax.random.normal(jax.random.fold_in(_gk, 15), (100000, 4), jnp.float32)
        edge_type_16 = jax.random.randint(jax.random.fold_in(_gk, 17), (100000,), 0, 16, jnp.int32)
        edge_type_64 = jax.random.randint(jax.random.fold_in(_gk, 18), (100000,), 0, 64, jnp.int32)
        edge_weight1 = jax.random.uniform(jax.random.fold_in(_gk, 19), (100000, 1), jnp.float32, 0.0, 0.999998)
        node_vec1 = jax.random.uniform(jax.random.fold_in(_gk, 20), (6250, 1), jnp.float32, 0.0, 1)
        return (x, src, dst, edge_attr_10, edge_attr_256, edge_attr_4, edge_type_16, edge_type_64, edge_weight1, node_vec1)
    x, src, dst, edge_attr_10, edge_attr_256, edge_attr_4, edge_type_16, edge_type_64, edge_weight1, node_vec1 = _rec_inputs()

    def _L0_gnn_setup():
        import jax, jax.numpy as jnp
        import numpy as np
        N_NODES = 2500
        N_EDGES = 40000
        NUM_RELS = 16
        IN_FEAT = 256
        OUT_FEAT = 256
        key = jax.random.key(seed)
        k_h, k_w, k_n, k_s, k_d, k_r = jax.random.split(key, 6)
        h = jax.random.normal(k_h, (N_NODES, IN_FEAT), dtype=jnp.float32)
        weight = jax.random.normal(k_w, (NUM_RELS, IN_FEAT, OUT_FEAT), dtype=jnp.float32)
        norm = jax.random.uniform(k_n, (N_EDGES, 1), dtype=jnp.float32)
        src = jax.random.randint(k_s, (N_EDGES,), 0, N_NODES, dtype=jnp.int32)
        dst = jax.random.randint(k_d, (N_EDGES,), 0, N_NODES, dtype=jnp.int32)
        rel_type = jax.random.randint(k_r, (N_EDGES,), 0, NUM_RELS, dtype=jnp.int32)
        return {'h': h, 'weight': weight, 'norm': norm, 'src': src, 'dst': dst, 'rel_type': rel_type}
    _L0_gnn_all = _L0_gnn_setup()
    _L0_gnn_in = {k: v for k, v in _L0_gnn_all.items() if k in ('weight',)}
    del _L0_gnn_all

    def _L1_gnn_setup():
        import jax, jax.numpy as jnp
        import numpy as np
        N_NODES = 6250
        N_EDGES = 100000
        DIM = 256
        EPS = 1e-06
        key = jax.random.key(seed)
        k1, k2, k3, k4, k5, k6, k7 = jax.random.split(key, 7)
        node_features = jax.random.normal(k1, (N_NODES, DIM), dtype=jnp.float32)
        edge_features = jax.random.normal(k2, (N_EDGES, DIM), dtype=jnp.float32)
        edge_index = jax.random.randint(k3, (2, N_EDGES), 0, N_NODES, dtype=jnp.int32)
        d_in_msg = 3 * DIM
        W_msg = jax.random.normal(k4, (d_in_msg, DIM), dtype=jnp.float32) / np.sqrt(d_in_msg)
        b_msg = jax.random.normal(k5, (DIM,), dtype=jnp.float32) * 0.01
        d_in_upd = 2 * DIM
        W_upd = jax.random.normal(k6, (d_in_upd, DIM), dtype=jnp.float32) / np.sqrt(d_in_upd)
        b_upd = jax.random.normal(k7, (DIM,), dtype=jnp.float32) * 0.01
        return {'node_features': node_features, 'edge_features': edge_features, 'edge_index': edge_index, 'W_msg': W_msg, 'b_msg': b_msg, 'W_upd': W_upd, 'b_upd': b_upd}
    _L1_gnn_all = _L1_gnn_setup()
    _L1_gnn_in = {k: v for k, v in _L1_gnn_all.items() if k in ('W_msg', 'b_msg', 'W_upd', 'b_upd')}
    del _L1_gnn_all

    def _L2_gnn_setup():
        import jax, jax.numpy as jnp
        import numpy as np
        N_NODES = 6250
        N_EDGES = 62500
        IN_DIM = 256
        HID = 64
        HEADS = 4
        N_REL = 64
        key = jax.random.key(seed)
        ks = jax.random.split(key, 16)
        s = 0.02
        return {'node_features': jax.random.normal(ks[0], (N_NODES, IN_DIM), jnp.float32), 'edge_index': jax.random.randint(ks[1], (2, N_EDGES), 0, N_NODES, jnp.int32), 'edge_relations': jax.random.randint(ks[2], (N_EDGES,), 0, N_REL, jnp.int32), 'query_emb': jax.random.normal(ks[3], (IN_DIM,), jnp.float32), 'Wq': jax.random.normal(ks[4], (IN_DIM, HID * HEADS), jnp.float32) * s, 'bq': jnp.zeros((HID * HEADS,), jnp.float32), 'Wk': jax.random.normal(ks[5], (IN_DIM, HID * HEADS), jnp.float32) * s, 'bk': jnp.zeros((HID * HEADS,), jnp.float32), 'Wv': jax.random.normal(ks[6], (IN_DIM, HID * HEADS), jnp.float32) * s, 'bv': jnp.zeros((HID * HEADS,), jnp.float32), 'rel_w': jax.random.normal(ks[7], (N_REL, HID), jnp.float32) * s, 'Wo': jax.random.normal(ks[8], (HID * HEADS, IN_DIM), jnp.float32) * s, 'bo': jnp.zeros((IN_DIM,), jnp.float32), 'gamma': jnp.ones((IN_DIM,), jnp.float32), 'beta': jnp.zeros((IN_DIM,), jnp.float32)}
    _L2_gnn_all = _L2_gnn_setup()
    _L2_gnn_in = {k: v for k, v in _L2_gnn_all.items() if k in ('query_emb', 'Wq', 'bq', 'Wk', 'bk', 'Wv', 'bv', 'rel_w', 'Wo', 'bo', 'gamma', 'beta')}
    del _L2_gnn_all

    def _L3_gnn_setup():
        import jax, jax.numpy as jnp
        import numpy as np
        import math
        N_NODES = 2500
        N_EDGES = 40000
        MUL = 64
        N_BASIS = 10
        N_HID = 100
        W_NUMEL = 4 * MUL

        def _split(x):
            s = x[..., :MUL]
            v = x[..., MUL:].reshape(x.shape[:-1] + (MUL, 3))
            return (s, v)

        def _fctp(s, v, W0, W1, attr, fan_in):
            inv = 1.0 / math.sqrt(fan_in)
            o0 = jnp.einsum('nu,uk->nk', s, W0) * attr * inv
            o1 = jnp.einsum('num,uk->nkm', v, W1) * attr[..., None] * inv
            return (o0, o1)
        key = jax.random.key(seed)
        ks = jax.random.split(key, 16)
        node_input = jax.random.normal(ks[0], (N_NODES, 4 * MUL), dtype=jnp.float32)
        node_attr = jnp.ones((N_NODES, 1), dtype=jnp.float32)
        node_deg = jax.random.randint(ks[1], (N_NODES, 1), 1, 33).astype(jnp.float32)
        edge_src = jax.random.randint(ks[2], (N_EDGES,), 0, N_NODES)
        edge_dst = jax.random.randint(ks[3], (N_EDGES,), 0, N_NODES)
        edge_attr = jax.random.normal(ks[4], (N_EDGES, 4), dtype=jnp.float32)
        edge_length_embedded = jax.random.uniform(ks[5], (N_EDGES, N_BASIS), dtype=jnp.float32)
        W_li0 = jax.random.normal(ks[6], (MUL, MUL), dtype=jnp.float32)
        W_li1 = jax.random.normal(ks[7], (MUL, MUL), dtype=jnp.float32)
        W_lm0 = jax.random.normal(ks[8], (MUL, MUL), dtype=jnp.float32)
        W_lm1 = jax.random.normal(ks[9], (MUL, MUL), dtype=jnp.float32)
        W_mlp1 = jax.random.normal(ks[10], (N_BASIS, N_HID), dtype=jnp.float32)
        W_mlp2 = jax.random.normal(ks[11], (N_HID, W_NUMEL), dtype=jnp.float32)
        W_lo0 = jax.random.normal(ks[12], (2 * MUL, MUL), dtype=jnp.float32)
        W_lo1 = jax.random.normal(ks[13], (2 * MUL, MUL), dtype=jnp.float32)
        return dict(node_input=node_input, node_attr=node_attr, node_deg=node_deg, edge_attr=edge_attr, edge_length_embedded=edge_length_embedded, W_li0=W_li0, W_li1=W_li1, W_lm0=W_lm0, W_lm1=W_lm1, W_mlp1=W_mlp1, W_mlp2=W_mlp2, W_lo0=W_lo0, W_lo1=W_lo1, edge_src=edge_src, edge_dst=edge_dst)
    _L3_gnn_all = _L3_gnn_setup()
    _L3_gnn_in = {k: v for k, v in _L3_gnn_all.items() if k in ('W_li0', 'W_li1', 'W_lm0', 'W_lm1', 'W_mlp1', 'W_mlp2', 'W_lo0', 'W_lo1')}
    del _L3_gnn_all
    return {'x': x, 'src': src, 'dst': dst, 'edge_attr_10': edge_attr_10, 'edge_attr_256': edge_attr_256, 'edge_attr_4': edge_attr_4, 'edge_type_16': edge_type_16, 'edge_type_64': edge_type_64, 'edge_weight1': edge_weight1, 'node_vec1': node_vec1, 'L0_gnn_weight': _L0_gnn_in['weight'], 'L1_gnn_W_msg': _L1_gnn_in['W_msg'], 'L1_gnn_b_msg': _L1_gnn_in['b_msg'], 'L1_gnn_W_upd': _L1_gnn_in['W_upd'], 'L1_gnn_b_upd': _L1_gnn_in['b_upd'], 'L2_gnn_query_emb': _L2_gnn_in['query_emb'], 'L2_gnn_Wq': _L2_gnn_in['Wq'], 'L2_gnn_bq': _L2_gnn_in['bq'], 'L2_gnn_Wk': _L2_gnn_in['Wk'], 'L2_gnn_bk': _L2_gnn_in['bk'], 'L2_gnn_Wv': _L2_gnn_in['Wv'], 'L2_gnn_bv': _L2_gnn_in['bv'], 'L2_gnn_rel_w': _L2_gnn_in['rel_w'], 'L2_gnn_Wo': _L2_gnn_in['Wo'], 'L2_gnn_bo': _L2_gnn_in['bo'], 'L2_gnn_gamma': _L2_gnn_in['gamma'], 'L2_gnn_beta': _L2_gnn_in['beta'], 'L3_gnn_W_li0': _L3_gnn_in['W_li0'], 'L3_gnn_W_li1': _L3_gnn_in['W_li1'], 'L3_gnn_W_lm0': _L3_gnn_in['W_lm0'], 'L3_gnn_W_lm1': _L3_gnn_in['W_lm1'], 'L3_gnn_W_mlp1': _L3_gnn_in['W_mlp1'], 'L3_gnn_W_mlp2': _L3_gnn_in['W_mlp2'], 'L3_gnn_W_lo0': _L3_gnn_in['W_lo0'], 'L3_gnn_W_lo1': _L3_gnn_in['W_lo1']}

def reference(x, src, dst, edge_attr_10, edge_attr_256, edge_attr_4, edge_type_16, edge_type_64, edge_weight1, node_vec1, L0_gnn_weight, L1_gnn_W_msg, L1_gnn_b_msg, L1_gnn_W_upd, L1_gnn_b_upd, L2_gnn_query_emb, L2_gnn_Wq, L2_gnn_bq, L2_gnn_Wk, L2_gnn_bk, L2_gnn_Wv, L2_gnn_bv, L2_gnn_rel_w, L2_gnn_Wo, L2_gnn_bo, L2_gnn_gamma, L2_gnn_beta, L3_gnn_W_li0, L3_gnn_W_li1, L3_gnn_W_lm0, L3_gnn_W_lm1, L3_gnn_W_mlp1, L3_gnn_W_mlp2, L3_gnn_W_lo0, L3_gnn_W_lo1):
    import jax
    import jax.numpy as jnp

    def _L0_gnn_ref(h, weight, norm, src, dst, rel_type):
        import jax, jax.numpy as jnp
        import numpy as np
        N_NODES = 2500
        N_EDGES = 40000
        NUM_RELS = 16
        IN_FEAT = 256
        OUT_FEAT = 256
        transformed = jnp.einsum('ni,rio->rno', h, weight)
        msg = transformed[rel_type, src] * norm
        out = jax.ops.segment_sum(msg, dst, num_segments=h.shape[0])
        return out

    def _L1_gnn_ref(node_features, edge_features, edge_index, W_msg, b_msg, W_upd, b_upd):
        import jax, jax.numpy as jnp
        import numpy as np
        N_NODES = 6250
        N_EDGES = 100000
        DIM = 256
        EPS = 1e-06
        row, col = (edge_index[0], edge_index[1])
        src = node_features[row]
        dst = node_features[col]
        msg_in = jnp.concatenate([src, dst, edge_features], axis=-1)
        messages = jax.nn.relu(msg_in @ W_msg + b_msg)
        n = node_features.shape[0]
        aggregated = jax.ops.segment_sum(messages, col, num_segments=n)
        counts = jax.ops.segment_sum(jnp.ones((col.shape[0], 1), jnp.float32), col, num_segments=n)
        aggregated = aggregated / (counts + EPS)
        upd_in = jnp.concatenate([node_features, aggregated], axis=-1)
        updated = jax.nn.relu(upd_in @ W_upd + b_upd)
        return updated

    def _L2_gnn_ref(node_features, edge_index, edge_relations, query_emb, Wq, bq, Wk, bk, Wv, bv, rel_w, Wo, bo, gamma, beta):
        import jax, jax.numpy as jnp
        import numpy as np
        N_NODES = 6250
        N_EDGES = 62500
        IN_DIM = 256
        HID = 64
        HEADS = 4
        N_REL = 64
        N = node_features.shape[0]
        D = rel_w.shape[1]
        H = Wq.shape[1] // D
        enh = node_features + 0.1 * query_emb[None, :]
        Q = (enh @ Wq + bq).reshape(N, H, D)
        K = (enh @ Wk + bk).reshape(N, H, D)
        V = (enh @ Wv + bv).reshape(N, H, D)
        src, dst = (edge_index[0], edge_index[1])
        rel = rel_w[edge_relations]
        mod_k = K[src] + 0.2 * rel[:, None, :]
        scores = jnp.einsum('ehd,ehd->eh', Q[dst], mod_k) / D ** 0.5
        seg_max = jax.ops.segment_max(scores, dst, num_segments=N)
        ex = jnp.exp(scores - seg_max[dst])
        denom = jax.ops.segment_sum(ex, dst, num_segments=N)
        w = ex / denom[dst]
        agg = jax.ops.segment_sum(w[:, :, None] * V[src], dst, num_segments=N)
        deg = jax.ops.segment_sum(jnp.ones((src.shape[0],), jnp.float32), dst, num_segments=N)
        msgs = jnp.where(deg[:, None, None] > 0, agg, V)
        out = msgs.reshape(N, H * D) @ Wo + bo
        x = out + node_features
        mu = jnp.mean(x, axis=-1, keepdims=True)
        var = jnp.var(x, axis=-1, keepdims=True)
        return (x - mu) / jnp.sqrt(var + 1e-05) * gamma + beta

    def _L3_gnn_ref(node_input, node_attr, node_deg, edge_attr, edge_length_embedded, W_li0, W_li1, W_lm0, W_lm1, W_mlp1, W_mlp2, W_lo0, W_lo1, edge_src, edge_dst):
        import jax, jax.numpy as jnp
        import numpy as np
        import math
        N_NODES = 2500
        N_EDGES = 40000
        MUL = 64
        N_BASIS = 10
        N_HID = 100
        W_NUMEL = 4 * MUL

        def _split(x):
            s = x[..., :MUL]
            v = x[..., MUL:].reshape(x.shape[:-1] + (MUL, 3))
            return (s, v)

        def _fctp(s, v, W0, W1, attr, fan_in):
            inv = 1.0 / math.sqrt(fan_in)
            o0 = jnp.einsum('nu,uk->nk', s, W0) * attr * inv
            o1 = jnp.einsum('num,uk->nkm', v, W1) * attr[..., None] * inv
            return (o0, o1)
        N = node_input.shape[0]
        x0, x1 = _split(node_input)
        f0, f1 = _fctp(x0, x1, W_li0, W_li1, node_attr, MUL)
        deg_isqrt = 1.0 / jnp.sqrt(node_deg)
        f0 = f0 * deg_isqrt
        f1 = f1 * deg_isqrt[..., None]
        m0, m1 = _fctp(x0, x1, W_lm0, W_lm1, node_attr, MUL)
        h = jax.nn.silu(edge_length_embedded @ W_mlp1 / math.sqrt(N_BASIS))
        ew = h @ W_mlp2 / math.sqrt(N_HID)
        wa, wb, wc, wd = (ew[:, :MUL], ew[:, MUL:2 * MUL], ew[:, 2 * MUL:3 * MUL], ew[:, 3 * MUL:])
        g0 = f0[edge_src]
        g1 = f1[edge_src]
        y0 = edge_attr[:, 0]
        y1 = edge_attr[:, 1:4]
        m0a = wa * g0 * y0[:, None]
        m0b = wb * jnp.einsum('eum,em->eu', g1, y1) / math.sqrt(3.0)
        m1a = wc[:, :, None] * g0[:, :, None] * y1[:, None, :]
        m1b = wd[:, :, None] * g1 * y0[:, None, None]
        s_mid = jax.ops.segment_sum(jnp.concatenate([m0a, m0b], axis=1), edge_dst, num_segments=N)
        v_mid = jax.ops.segment_sum(jnp.concatenate([m1a, m1b], axis=1), edge_dst, num_segments=N)
        s_mid = s_mid * deg_isqrt
        v_mid = v_mid * deg_isqrt[..., None]
        o0, o1 = _fctp(s_mid, v_mid, W_lo0, W_lo1, node_attr, 2 * MUL)
        c_s, c_x = (math.sin(math.pi / 8), math.cos(math.pi / 8))
        out0 = c_s * m0 + c_x * o0
        out1 = c_s * m1 + c_x * o1
        return jnp.concatenate([out0, out1.reshape(N, 3 * MUL)], axis=1)
    edge_index = jnp.stack([src, dst])
    deg = jnp.maximum(jax.ops.segment_sum(jnp.ones(dst.shape, jnp.float32), dst, num_segments=6250), 1.0)
    x = _layernorm(x + _L0_gnn_ref(x, L0_gnn_weight, edge_weight1, src, dst, edge_type_16), axis=-1)
    x = _layernorm(x + _L1_gnn_ref(x, edge_attr_256, edge_index, L1_gnn_W_msg, L1_gnn_b_msg, L1_gnn_W_upd, L1_gnn_b_upd), axis=-1)
    x = _layernorm(x + _L2_gnn_ref(x, edge_index, edge_type_64, L2_gnn_query_emb, L2_gnn_Wq, L2_gnn_bq, L2_gnn_Wk, L2_gnn_bk, L2_gnn_Wv, L2_gnn_bv, L2_gnn_rel_w, L2_gnn_Wo, L2_gnn_bo, L2_gnn_gamma, L2_gnn_beta), axis=-1)
    x = _layernorm(x + _L3_gnn_ref(x, node_vec1, deg[:, None], edge_attr_4, edge_attr_10, L3_gnn_W_li0, L3_gnn_W_li1, L3_gnn_W_lm0, L3_gnn_W_lm1, L3_gnn_W_mlp1, L3_gnn_W_mlp2, L3_gnn_W_lo0, L3_gnn_W_lo1, src, dst), axis=-1)
    return x

_drawn_inputs = setup_inputs


def setup_inputs(seed=0):
    import zlib

    import numpy as np

    out = dict(_drawn_inputs(seed))
    spreads = {'L2_gnn_bq': (0.0, 0.8),
     'L2_gnn_bk': (0.0, 2.0),
     'L2_gnn_bv': (0.0, 0.478),
     'L2_gnn_bo': (0.0, 0.1),
     'L2_gnn_gamma': (1.0, 0.2),
     'L2_gnn_beta': (0.0, 0.1)}
    factors = {'edge_attr_10': 3.66,
     'L1_gnn_b_msg': 21.526,
     'L1_gnn_b_upd': 8.0,
     'L2_gnn_query_emb': 8.0,
     'L2_gnn_Wq': 8.0,
     'L2_gnn_Wk': 8.0,
     'L2_gnn_Wv': 3.191,
     'L2_gnn_rel_w': 64.0,
     'L3_gnn_W_lo0': 3.409}
    for name, (base, spread) in spreads.items():
        noise = np.random.default_rng([zlib.crc32(name.encode()), seed]).standard_normal(out[name].shape)
        drawn = base * np.exp(spread * noise) if base else spread * noise
        out[name] = jnp.asarray(drawn.astype(out[name].dtype))
    for name, factor in factors.items():
        out[name] = (out[name] * factor).astype(out[name].dtype)
    return out
```

```python
import concourse.bass as bass
from concourse import mybir
from contextlib import ExitStack

F32 = mybir.dt.float32
I32 = mybir.dt.int32
ALU = mybir.AluOpType
ACT = mybir.ActivationFunctionType
AX = mybir.AxisListType

N, E, D = 6250, 100000, 256
P = 128
NT = -(-N // P)
NLAST = N - (NT - 1) * P
GN = 7
NG = NT // GN
R, H, HD, NREL, NB, NHID, MUL = 16, 4, 64, 64, 10, 100, 64
U = 4
LOGU = 2
TC, TP = 7, 113
ET = TC * TP
PAD_NODE = 8191
BIG = 1024.0
NEG = -1.0e30
AW = D + H
assert NT == GN * NG and ET * P >= E + (U + 1) * P and U == 1 << LOGU


class Phase(ExitStack):

    def __init__(self, nc, name):
        super().__init__()
        self.nc, self.name, self.sems = nc, name, []

    def sb(self, name, shape, dt=F32):
        return self.enter_context(self.nc.sbuf_tensor(f"{self.name}_{name}", shape, dt))

    def ps(self, name):
        return self.enter_context(self.nc.psum_tensor(f"{self.name}_{name}", [P, 512], F32))

    def sem(self, name):
        self.sems.append(self.nc.alloc_semaphore(name=f"{self.name}_{name}"))
        return self.sems[-1]

    def __exit__(self, *error):
        super().__exit__(*error)
        if error[0] is None:
            self.nc.clear_and_free_semaphores(self.sems)
            self.nc.all_engine_barrier()


class Count:

    def __init__(self, eng, sem, turn=0, per_turn=0):
        self.eng, self.sem, self.start, self.per, self.n = eng, sem, turn * per_turn, per_turn, 0

    def then_wait(self, ins):
        self.n += 1
        ins.then_inc(self.sem, 1)
        self.eng.wait_ge(self.sem, self.start + self.n)

    def full(self):
        assert self.n == self.per, (self.n, self.per)


def window(eng, table, n):
    lo = eng.value_load(table[0:1, bass.ds(n, 1)], min_val=0, max_val=NT * ET)
    hi = eng.value_load(table[0:1, bass.ds(n + 1, 1)], min_val=0, max_val=NT * ET)
    off = eng.value_load(table[0:1, bass.ds(n + 64, 1)], min_val=-NT * ET * U, max_val=ET)
    return lo, hi, off


def edge_tile(nc, off, i, b):
    return nc.s_assert_within(off + i * U, 0, ET - U, skip_runtime_bounds_check_because="the table is clamped to it") + b


def buffer_of(j):
    return j % 2, (2 if j >= 2 else 1 if j == 0 else 3)


LAG = 3


def gnn(nc, x, src, dst, dst_rows, rel, norm, etype, y, node_attr, ea10, ea256,
        w0, w_msg, b_msg, w_upd, b_upd, q_emb, wq, bq, wk, bk, wv, bv, rel_w, wo, bo, gamma, beta,
        w_li0, w_li1, w_lm0, w_lm1, w_mlp1, w_mlp2, w_lo0, w_lo1,
        rel_rows, src_table, key_table, value_table, score_rows, out):
    with ExitStack() as ctx:
        def sb(name, shape, dt=F32):
            return ctx.enter_context(nc.sbuf_tensor(name, shape, dt))

        k = dict(
            X=sb("X", [P, NT, D]),
            node_area=sb("node_area", [P, NT * (AW + D)]),
            src_id=sb("src_id", [P, ET], I32),
            dstf=sb("dstf", [P, ET]),
            table=sb("table", [1, 128], I32),
            ident=sb("ident", [P, P]),
            node_col=sb("node_col", [P, P]),
            tile_base=sb("tile_base", [P, NT]),
            node_id=sb("node_id", [P, NT]),
            count=sb("count", [P, NT]),
            zeros=sb("zeros", [P, 512]),
        )
        k["isq"] = sb("isq", [P, NT])
        k["S"] = sb("S", [P, ET * H])
        k["M"] = sb("M", [P, NT * H])
        k["AGG"] = k["node_area"][:, 0:NT * AW].rearrange("p (n c) -> p n c", c=AW)
        k["NODE2"] = k["node_area"][:, NT * AW:NT * (AW + D)].rearrange("p (n c) -> p n c", c=D)
        k["AGG2"] = k["node_area"][:, 0:NT * 512].rearrange("p (n c) -> p n c", c=512)
        windows_phase(nc, k, x, src, dst, dst_rows)
        relation_transform(nc, k, w0, rel_rows)
        relation_edges(nc, k, rel, norm, rel_rows)
        message_tables(nc, k, w_msg, b_msg, src_table)
        message_edges(nc, k, ea256, w_msg, src_table)
        update_nodes(nc, k, w_upd, b_upd)
        attention_tables(nc, k, q_emb, wq, bq, wk, bk, wv, bv, key_table, value_table)
        score_edges(nc, k, etype, rel_w, key_table)
        greatest_scores(nc, k, dst_rows, score_rows)
        attention_edges(nc, k, value_table)
        attention_out(nc, k, wo, bo, value_table)
        affine_norm(nc, k, gamma, beta)
        product_tables(nc, k, node_attr, w_li0, w_li1, src_table)
        tensor_product_edges(nc, k, y, ea10, w_mlp1, w_mlp2, src_table)
        product_out(nc, k, node_attr, w_lm0, w_lm1, w_lo0, w_lo1)
        last_norm(nc, k, out)


def windows_phase(nc, k, x, src, dst, dst_rows):
    with Phase(nc, "w") as phase:
        sb, ps, sem = phase.sb, phase.ps, phase.sem
        dst_i = sb("dst_i", [P, ET], I32)
        rows_i = sb("rows_i", [TP, TC, P], I32)
        lo_hi = sb("lo_hi", [TP, 2, TC])
        tile_no = sb("tile_no", [TP, 2, TC])
        tmp = sb("tmp", [TP, 2, NT])
        cand = sb("cand", [TP, TC, 2, NT])
        best = sb("best", [TP, 2, NT])
        col = sb("col", [2 * NT, 1])
        row = sb("row", [1, 2, NT])
        turns = sb("turns", [1, 64])
        turns_i = sb("turns_i", [1, 64], I32)
        sum_a = sb("sum_a", [1, 128])
        sum_b = sb("sum_b", [1, 128])
        offs = sb("offs", [1, 64])
        ps = ps("ps_w")
        loaded_x, loaded_e, loaded_r = sem("loaded_x"), sem("loaded_e"), sem("loaded_r")
        made, ident_set, best_done, turned, col_done, row_done = (
            sem("made"), sem("ident_set"), sem("best_done"), sem("turned"), sem("col_done"), sem("row_done"))
        dve_step = sem("dve_step")
        with nc.Block() as block:
            @block.sync
            def _(sp):
                sp.dma_start(k["X"][:, 0:NT - 1, :], x[0:(NT - 1) * P, :].rearrange("(t p) d -> p t d", p=P)).then_inc(loaded_x, 16)
                sp.wait_ge(made, 1)
                sp.dma_start(k["X"][0:NLAST, NT - 1, :], x[(NT - 1) * P:N, :]).then_inc(loaded_x, 16)
                sp.wait_ge(loaded_x, 32)

            @block.scalar
            def _(act):
                act.dma_start(rows_i[:, :, :], dst_rows.rearrange("(c p) e -> p c e", p=TP)).then_inc(loaded_r, 16)
                act.dma_start(dst_i[:, :], dst).then_inc(loaded_e, 16)
                act.dma_start(k["src_id"][:, :], src).then_inc(loaded_e, 16)
                act.wait_ge(loaded_e, 32)

            @block.gpsimd
            def _(pool):
                nc.gpsimd.memset(k["X"][:, NT - 1, :], 0.0).then_inc(made, 1)
                iota = dict(allow_small_or_imprecise_dtypes=True)
                nc.gpsimd.memset(k["ident"][:, :], 0.0).then_inc(ident_set, 1)
                nc.gpsimd.memset(k["zeros"][:, :], 0.0).then_inc(made, 1)
                nc.gpsimd.iota(k["node_col"][:, :], pattern=[[1, P]], base=0, channel_multiplier=0, **iota).then_inc(made, 1)
                nc.gpsimd.iota(k["tile_base"][:, :], pattern=[[P, NT]], base=0, channel_multiplier=0, **iota).then_inc(made, 1)
                nc.gpsimd.iota(k["node_id"][:, :], pattern=[[P, NT]], base=0, channel_multiplier=1, **iota).then_inc(made, 1)
                nc.gpsimd.iota(tile_no[:, 0, :], pattern=[[-TP, TC]], base=int(BIG), channel_multiplier=-1, **iota).then_inc(made, 1)
                nc.gpsimd.iota(tile_no[:, 1, :], pattern=[[TP, TC]], base=1, channel_multiplier=1, **iota).then_inc(made, 1)
                pool.wait_ge(ident_set, 1)
                nc.gpsimd.affine_select(out=k["ident"][:, :], in_=k["ident"][:, :], compare_op=ALU.not_equal,
                                        fill=1.0, base=0, pattern=[[-1, P]], channel_multiplier=1).then_inc(made, 1)

            @block.tensor
            def _(pe):
                pe.wait_ge(best_done, 1)
                nc.tensor.transpose(ps[0:2 * NT, 0:TP], best[:, :, :].rearrange("p a n -> p (a n)"),
                                    k["ident"][0:TP, 0:TP]).then_inc(turned, 1)
                pe.wait_ge(col_done, 1)
                nc.tensor.transpose(ps[0:1, 256:256 + 2 * NT], col[:, :], k["ident"][0:2 * NT, 0:2 * NT]).then_inc(turned, 1)

            @block.vector
            def _(dve):
                step = Count(dve, dve_step)
                dve.wait_ge(made, 8)
                dve.wait_ge(loaded_e, 32)
                nc.vector.tensor_copy(k["dstf"][:, :], dst_i[:, :])
                dve.wait_ge(loaded_r, 16)
                step.then_wait(nc.vector.tensor_reduce(lo_hi[:, 0, :], rows_i[:, :, :], AX.X, ALU.min))
                step.then_wait(nc.vector.tensor_reduce(lo_hi[:, 1, :], rows_i[:, :, :], AX.X, ALU.max))
                step.then_wait(nc.vector.tensor_scalar(lo_hi[:, 0, :], lo_hi[:, 0, :], -float(P - 1), None, ALU.add))
                base = k["tile_base"]
                for c in range(TC):
                    step.then_wait(nc.vector.tensor_scalar(tmp[:, 0, :], base[0:TP, :], lo_hi[:, 1, c:c + 1], None, ALU.is_le))
                    step.then_wait(nc.vector.scalar_tensor_tensor(tmp[:, 1, :], base[0:TP, :], lo_hi[:, 0, c:c + 1], tmp[:, 0, :], ALU.is_ge, ALU.mult))
                    for a in range(2):
                        step.then_wait(nc.vector.tensor_scalar(cand[:, c, a, :], tmp[:, 1, :], tile_no[:, a, c:c + 1], None, ALU.mult))
                nc.vector.tensor_reduce(best[:, :, :], cand[:, :, :, :].rearrange("p c a n -> p a n c"), AX.X, ALU.max).then_inc(best_done, 1)
                dve.wait_ge(turned, 1)
                nc.vector.tensor_reduce(col[:, :], ps[0:2 * NT, 0:TP], AX.X, ALU.max).then_inc(col_done, 1)
                dve.wait_ge(turned, 2)
                step.then_wait(nc.vector.tensor_copy(row[:, :, :].rearrange("p a n -> p (a n)"), ps[0:1, 256:256 + 2 * NT]))
                step.then_wait(nc.vector.tensor_scalar(row[:, 0, :], row[:, 0, :], -1.0, BIG, ALU.mult, ALU.add))
                step.then_wait(nc.vector.tensor_scalar(row[:, 0, :], row[:, 0, :], float(ET - U), None, ALU.min))
                step.then_wait(nc.vector.memset(turns[:, :], 0.0))
                step.then_wait(nc.vector.tensor_tensor(turns[:, 0:NT], row[:, 1, :], row[:, 0, :], ALU.subtract))
                step.then_wait(nc.vector.tensor_scalar(turns[:, 0:NT], turns[:, 0:NT], 1.0, float(U - 1), ALU.max, ALU.add))
                step.then_wait(nc.vector.tensor_copy(turns_i[:, :], turns[:, :]))
                step.then_wait(nc.vector.tensor_single_scalar(turns_i[:, :], turns_i[:, :], LOGU, op=ALU.arith_shift_right))
                step.then_wait(nc.vector.memset(sum_a[:, :], 0.0))
                step.then_wait(nc.vector.memset(sum_b[:, :], 0.0))
                step.then_wait(nc.vector.tensor_copy(sum_a[:, 65:128], turns_i[:, 0:63]))
                a, b = sum_a, sum_b
                for s in (1, 2, 4, 8, 16, 32):
                    step.then_wait(nc.vector.tensor_tensor(b[:, 64:128], a[:, 64:128], a[:, 64 - s:128 - s], ALU.add))
                    a, b = b, a
                step.then_wait(nc.vector.tensor_copy(k["table"][:, 0:64], a[:, 64:128]))
                step.then_wait(nc.vector.memset(offs[:, :], 0.0))
                step.then_wait(nc.vector.scalar_tensor_tensor(offs[:, 0:NT], a[:, 64:64 + NT], -float(U), row[:, 0, :], ALU.mult, ALU.add))
                step.then_wait(nc.vector.tensor_copy(k["table"][:, 64:128], offs[:, :]))


def relation_transform(nc, k, w0, rel_rows):
    with Phase(nc, "rt") as phase:
        sb, ps, sem = phase.sb, phase.ps, phase.sem
        RW = R * D
        W = k["node_area"][:, 0:2 * RW].rearrange("p (c r) -> p c r", c=2)
        stage = k["node_area"][:, 2 * RW:4 * RW].rearrange("p (c r) -> p c r", c=2)
        xT = sb("xT", [P, 2, 2, P])
        xs = sb("xs", [P, 2, D])
        xs_ready, slot_seen = sem("xs_ready"), sem("slot_seen")
        ps_t = [ps(f"ps_t{b}") for b in range(2)]
        ps_o = [ps(f"ps_o{b}") for b in range(4)]
        w_loaded, turned, xT_ready, xT_free = sem("w_loaded"), sem("turned"), sem("xT_ready"), sem("xT_free")
        made = [sem(f"made{c}") for c in range(4)]
        taken = [sem(f"taken{c}") for c in range(4)]
        stored, stage_free = sem("stored"), sem("stage_free")
        CH = RW // 512
        with nc.Block() as block:
            @block.sync
            def _(sp):
                for c in range(2):
                    sp.dma_start(W[:, c, :].rearrange("p (r o) -> p r o", r=R), w0[:, c * P:(c + 1) * P, :].rearrange("r p o -> p r o")).then_inc(w_loaded, 16)
                sp.sem_inc(stage_free, LAG)
                with sp.Fori(0, NG) as g:
                    for j in range(GN):
                        b, _ = buffer_of(j)
                        for c in range(4):
                            sp.wait_ge(taken[c], (g * GN + j + 1) * (CH // 4) + 1)
                        sp.dma_start(rel_rows[bass.ds((g * GN + j) * P, P), :], stage[:, b, :]).then_inc(stored, 16)
                        sp.wait_ge(stored, (g * GN + j) * 16 + 16)
                        sp.sem_inc(stage_free, 1)

            @block.gpsimd
            def _(pool):
                with pool.Fori(0, NG) as g:
                    for j in range(GN):
                        b, back = buffer_of(j)
                        pool.wait_ge(turned, g * GN + j - back + 1 + LAG)
                        pool.sem_inc(slot_seen, 1)
                        nc.gpsimd.tensor_copy(xs[:, b, :], k["X"][:, bass.ds(g * GN + j, 1), :].rearrange("p a d -> p (a d)")).then_inc(xs_ready, 1)

            def taker(eng, copy, cs):
                for c in cs:
                    eng.sem_inc(taken[c], 1)
                with eng.Fori(0, NG) as g:
                    for j in range(GN):
                        b, back = buffer_of(j)
                        if eng is not nc.vector:
                            eng.wait_ge(turned, g * GN + j + 1 + LAG)
                            copy(xT[:, b, :, :].rearrange("p c n -> p (c n)"), ps_t[b][:, 0:2 * P]).then_inc(xT_ready, 1)
                        for q in range(CH // 4):
                            for c in cs:
                                if q == 0 and c == cs[0]:
                                    eng.wait_ge(stage_free, g * GN + j - back + 1 + LAG)
                                eng.wait_ge(made[c], (g * GN + j) * (CH // 4) + q + 1)
                                ch = 4 * q + c
                                copy(stage[:, b, ch * 512:(ch + 1) * 512], ps_o[c][:, :]).then_inc(taken[c], 1)

            @block.scalar
            def _(act):
                taker(act, nc.scalar.copy, (1, 3))

            @block.vector
            def _(dve):
                taker(dve, nc.vector.tensor_copy, (0, 2))

            @block.tensor
            def _(pe):
                pe.sem_inc(turned, LAG)
                pe.wait_ge(w_loaded, 32)
                with pe.Fori(0, NG) as g:
                    for j in range(GN):
                        b, _ = buffer_of(j)
                        pe.wait_ge(xs_ready, g * GN + j + 1)
                        for c in range(2):
                            ins = nc.tensor.transpose(ps_t[b][:, c * P:(c + 1) * P], xs[:, b, c * P:(c + 1) * P], k["ident"][:, :])
                        ins.then_inc(turned, 1)
                        pe.wait_ge(xT_ready, g * GN + j + 1)
                        for ch in range(CH):
                            pe.wait_ge(taken[ch % 4], (g * GN + j) * (CH // 4) + ch // 4 + 1)
                            for c in range(2):
                                ins = nc.tensor.matmul(ps_o[ch % 4][:, :], xT[:, b, c, :], W[:, c, ch * 512:(ch + 1) * 512], start=(c == 0), stop=(c == 1))
                            ins.then_inc(made[ch % 4], 1)


def gather_turn(nc, pool, idx, ids, rows, table_rows, t, b, s, free, free_seen, idx_set, idx_seen, gathered):
    pool.wait_ge(free, s + 1)
    pool.sem_inc(free_seen, 1)
    nc.gpsimd.tensor_copy(idx[:, b:b + 1], ids[:, bass.ds(t, 1)]).then_inc(idx_set, 1)
    pool.wait_ge(idx_set, s + 1)
    pool.sem_inc(idx_seen, 1)
    pool.indirect_dma_start(out=rows[:, b, :], out_offset=None, in_=table_rows,
                            in_offset=bass.IndirectOffsetOnAxis(ap=idx[:, b:b + 1], axis=0)).then_inc(gathered[b], 16)


def relation_edges(nc, k, rel, norm, rel_rows):
    with Phase(nc, "re") as phase:
        sb, ps, sem = phase.sb, phase.ps, phase.sem
        row_id = sb("row_id", [P, ET], I32)
        rel_sb = sb("rel_sb", [P, ET], I32)
        norm_sb = sb("norm_sb", [P, ET])
        idx = sb("idx", [P, U], I32)
        rows = sb("rows", [P, U, D])
        pick = sb("pick", [P, U, P])
        cols = sb("cols", [P, P])
        acc = ps("acc")
        loaded, ids_made, idx_set, idx_seen, free_seen = (sem(n) for n in ("loaded", "ids_made", "idx_set", "idx_seen", "free_seen"))
        gathered = [sem(f"gathered{b}") for b in range(U)]
        picked, cols_set, cols_seen, summed, acc_done, acc_free, dve_step = (
            sem("picked"), sem("cols_set"), sem("cols_seen"), sem("summed"), sem("acc_done"), sem("acc_free"), sem("dve_step"))
        with nc.Block() as block:
            @block.sync
            def _(sp):
                sp.dma_start(rel_sb[:, :], rel).then_inc(loaded, 16)
                sp.dma_start(norm_sb[:, :], norm).then_inc(loaded, 16)

            @block.gpsimd
            def _(pool):
                pool.wait_ge(ids_made, 1)
                with pool.Fori(0, NT) as n:
                    lo, hi, off = window(pool, k["table"], n)
                    with pool.Fori(lo, hi) as i:
                        for b in range(U):
                            gather_turn(nc, pool, idx, row_id, rows, rel_rows.rearrange("n (r d) -> (n r) d", r=R), edge_tile(nc, off, i, b), b, i * U + b,
                                        summed, free_seen, idx_set, idx_seen, gathered)

            @block.vector
            def _(dve):
                step = Count(dve, dve_step)
                dve.wait_ge(loaded, 32)
                step.then_wait(nc.vector.tensor_scalar(row_id[:, :], k["src_id"][:, :], float(R), None, ALU.mult))
                nc.vector.tensor_tensor(row_id[:, :], row_id[:, :], rel_sb[:, :], ALU.add).then_inc(ids_made, 1)
                dve.wait_ge(ids_made, 1)
                with dve.Fori(0, NT) as n:
                    lo, hi, off = window(dve, k["table"], n)
                    nc.vector.tensor_scalar(cols[:, :], k["node_col"][:, :], k["tile_base"][:, bass.ds(n, 1)], None, ALU.add).then_inc(cols_set, 1)
                    dve.wait_ge(cols_set, n + 1)
                    dve.sem_inc(cols_seen, 1)
                    with dve.Fori(lo, hi) as i:
                        for b in range(U):
                            t = edge_tile(nc, off, i, b)
                            dve.wait_ge(summed, i * U + b + 1)
                            nc.vector.tensor_scalar(pick[:, b, :], cols[:, :], k["dstf"][:, bass.ds(t, 1)], norm_sb[:, bass.ds(t, 1)],
                                                    ALU.is_equal, ALU.mult).then_inc(picked, 1)
                    dve.wait_ge(picked, hi * U)
                    dve.sem_inc(cols_seen, 1)

            @block.tensor
            def _(pe):
                pe.sem_inc(summed, U)
                with pe.Fori(0, NT) as n:
                    lo, hi, off = window(pe, k["table"], n)
                    pe.wait_ge(acc_free, n + 1)
                    nc.tensor.matmul(acc[:, 0:D], k["zeros"][0:1, 0:P], k["zeros"][0:1, 0:D], start=True, stop=False)
                    with pe.Fori(lo, hi) as i:
                        for b in range(U):
                            pe.wait_ge(picked, i * U + b + 1)
                            pe.wait_ge(gathered[b], i * 16 + 16)
                            nc.tensor.matmul(acc[:, 0:D], pick[:, b, :], rows[:, b, :], start=False, stop=False).then_inc(summed, 1)
                    nc.tensor.matmul(acc[:, 0:D], k["zeros"][0:1, 0:P], k["zeros"][0:1, 0:D], start=False, stop=True).then_inc(acc_done, 1)

            @block.scalar
            def _(act):
                act.sem_inc(acc_free, 1)
                with act.Fori(0, NT) as n:
                    act.wait_ge(acc_done, n + 1)
                    nc.scalar.copy(k["AGG"][:, bass.ds(n, 1), 0:D].rearrange("p a d -> p (a d)"), acc[:, 0:D]).then_inc(acc_free, 1)


def message_edges(nc, k, ea256, w_msg, src_table):
    with Phase(nc, "me") as phase:
        sb, ps, sem = phase.sb, phase.ps, phase.sem
        W = sb("W", [P, 2, D])
        idx = sb("idx", [P, U], I32)
        rows = sb("rows", [P, U, D])
        edge_T = sb("edge_T", [P, U, 2, P])
        pick = sb("pick", [P, U, P])
        pick_T = sb("pick_T", [P, U, P])
        pre = sb("pre", [P, U, D])
        msg = sb("msg", [P, U, D + 1])
        cols = sb("cols", [P, P])
        acc = ps("acc")
        ps_t = [ps("ps_t0"), ps("ps_t1")]
        ps_e = [ps(f"ps_e{b}") for b in range(U)]
        w_loaded, ones_set = sem("w_loaded"), sem("ones_set")
        gathered = [sem(f"gathered{b}") for b in range(U)]
        loaded = [sem(f"loaded{b}") for b in range(U)]
        idx_set, idx_seen, rows_free, free_seen, edge_free = (sem(n) for n in ("idx_set", "idx_seen", "rows_free", "free_seen", "edge_free"))
        cols_set, cols_seen, picked, turned, pick_T_ready = (sem(n) for n in ("cols_set", "cols_seen", "picked", "turned", "pick_T_ready"))
        made, pre_ready, msg_ready, summed, acc_done, acc_free = (sem(n) for n in ("made", "pre_ready", "msg_ready", "summed", "acc_done", "acc_free"))
        with nc.Block() as block:
            @block.sync
            def _(sp):
                sp.dma_start(W[:, :, :], w_msg[2 * D:3 * D, :].rearrange("(c p) o -> p c o", p=P)).then_inc(w_loaded, 16)
                with sp.Fori(0, NT) as n:
                    lo, hi, off = window(sp, k["table"], n)
                    with sp.Fori(lo, hi) as i:
                        for b in range(U):
                            sp.wait_ge(edge_free, i * U + b + 1)
                            sp.dma_start(edge_T[:, b, :, :].rearrange("p c e -> p (c e)"),
                                         ea256[bass.ds(edge_tile(nc, off, i, b), 1), :, :, :].rearrange("a p c e -> (a p) (c e)")).then_inc(loaded[b], 16)

            @block.gpsimd
            def _(pool):
                with pool.Fori(0, NT) as n:
                    lo, hi, off = window(pool, k["table"], n)
                    with pool.Fori(lo, hi) as i:
                        for b in range(U):
                            gather_turn(nc, pool, idx, k["src_id"], rows, src_table, edge_tile(nc, off, i, b), b, i * U + b,
                                        rows_free, free_seen, idx_set, idx_seen, gathered)

            @block.vector
            def _(dve):
                dve.sem_inc(rows_free, U)
                nc.vector.memset(msg[:, :, D:D + 1], 1.0).then_inc(ones_set, 1)
                with dve.Fori(0, NT) as n:
                    lo, hi, off = window(dve, k["table"], n)
                    nc.vector.tensor_scalar(cols[:, :], k["node_col"][:, :], k["tile_base"][:, bass.ds(n, 1)], None, ALU.add).then_inc(cols_set, 1)
                    dve.wait_ge(cols_set, n + 1)
                    dve.sem_inc(cols_seen, 1)
                    with dve.Fori(lo, hi) as i:
                        for b in range(U):
                            dve.wait_ge(summed, i * U + b + 1)
                            nc.vector.tensor_scalar(pick[:, b, :], cols[:, :], k["dstf"][:, bass.ds(edge_tile(nc, off, i, b), 1)], None,
                                                    ALU.is_equal).then_inc(picked, 1)
                        for b in range(U):
                            dve.wait_ge(gathered[b], i * 16 + 16)
                            dve.wait_ge(made, i * U + b + 1)
                            nc.vector.tensor_tensor(pre[:, b, :], ps_e[b][:, 0:D], rows[:, b, :], ALU.add).then_inc(rows_free, 1)
                    dve.wait_ge(picked, hi * U)
                    dve.sem_inc(cols_seen, 1)

            @block.scalar
            def _(act):
                act.sem_inc(acc_free, 1)
                with act.Fori(0, NT) as n:
                    lo, hi, off = window(act, k["table"], n)
                    with act.Fori(lo, hi) as i:
                        def turn_pick(b):
                            act.wait_ge(turned, i * U + b + 1)
                            nc.scalar.copy(pick_T[:, b, :], ps_t[b % 2][:, 0:P]).then_inc(pick_T_ready, 1)
                        turn_pick(0)
                        for b in range(U):
                            if b + 1 < U:
                                turn_pick(b + 1)
                            act.wait_ge(rows_free, i * U + b + 1 + U)
                            nc.scalar.activation(msg[:, b, 0:D], pre[:, b, :], ACT.Relu).then_inc(msg_ready, 1)
                    act.wait_ge(acc_done, n + 1)
                    nc.scalar.copy(k["AGG"][:, bass.ds(n, 1), 0:D + 1].rearrange("p a d -> p (a d)"), acc[:, 0:D + 1]).then_inc(acc_free, 1)

            @block.tensor
            def _(pe):
                pe.sem_inc(summed, U)
                pe.sem_inc(edge_free, U)
                pe.wait_ge(w_loaded, 16)
                pe.wait_ge(ones_set, 1)
                with pe.Fori(0, NT) as n:
                    lo, hi, off = window(pe, k["table"], n)
                    pe.wait_ge(acc_free, n + 1)
                    nc.tensor.matmul(acc[:, 0:D + 1], k["zeros"][0:1, 0:P], k["zeros"][0:1, 0:D + 1], start=True, stop=False)
                    with pe.Fori(lo, hi) as i:
                        def turn(b):
                            pe.wait_ge(picked, i * U + b + 1)
                            nc.tensor.transpose(ps_t[b % 2][:, 0:P], pick[:, b, :], k["ident"][:, :]).then_inc(turned, 1)

                        def add_up(b):
                            pe.wait_ge(msg_ready, i * U + b + 1)
                            nc.tensor.matmul(acc[:, 0:D + 1], pick[:, b, :], msg[:, b, :], start=False, stop=False).then_inc(summed, 1)
                        turn(0)
                        for b in range(U):
                            if b + 1 < U:
                                turn(b + 1)
                            pe.wait_ge(rows_free, i * U + b + 1)
                            pe.wait_ge(loaded[b], i * 16 + 16)
                            nc.tensor.matmul(ps_e[b][:, 0:D], edge_T[:, b, 0, :], W[:, 0, :], start=True, stop=False)
                            nc.tensor.matmul(ps_e[b][:, 0:D], edge_T[:, b, 1, :], W[:, 1, :], start=False, stop=False).then_inc(edge_free, 1)
                            pe.wait_ge(pick_T_ready, i * U + b + 1)
                            nc.tensor.matmul(ps_e[b][:, 0:D], pick_T[:, b, :], k["NODE2"][:, bass.ds(n, 1), :].rearrange("p a d -> p (a d)"),
                                             start=False, stop=True).then_inc(made, 1)
                            if b:
                                add_up(b - 1)
                        add_up(U - 1)
                    nc.tensor.matmul(acc[:, 0:D + 1], k["zeros"][0:1, 0:P], k["zeros"][0:1, 0:D + 1], start=False, stop=True).then_inc(acc_done, 1)


def score_edges(nc, k, etype, rel_w, key_table):
    with Phase(nc, "se") as phase:
        sb, ps, sem = phase.sb, phase.ps, phase.sem
        type_i = sb("type_i", [P, ET], I32)
        typef = sb("typef", [P, ET])
        rel_in = sb("rel_in", [P, HD])
        rel_sb = sb("rel_sb", [P, H, HD])
        idx = sb("idx", [P, U], I32)
        rows = sb("rows", [P, U, D])
        pick = sb("pick", [P, U, 2, P])
        pick_T = sb("pick_T", [P, U, 2, P])
        key = sb("key", [P, U, D])
        prod = sb("prod", [P, U, D])
        score = sb("score", [P, U, H])
        cols = sb("cols", [P, P])
        ps_t = [ps("ps_t0"), ps("ps_t1")]
        ps_q = [ps(f"ps_q{b}") for b in range(U)]
        loaded, rel_zeroed, rel_ready, s_zeroed = (sem(n) for n in ("loaded", "rel_zeroed", "rel_ready", "s_zeroed"))
        gathered = [sem(f"gathered{b}") for b in range(U)]
        idx_set, idx_seen, rows_free, free_seen = (sem(n) for n in ("idx_set", "idx_seen", "rows_free", "free_seen"))
        cols_set, cols_seen, picked, turned, pick_T_ready, made = (sem(n) for n in ("cols_set", "cols_seen", "picked", "turned", "pick_T_ready", "made"))
        multiplied, reduced, score_added = (sem(n) for n in ("multiplied", "reduced", "score_added"))
        with nc.Block() as block:
            @block.sync
            def _(sp):
                sp.dma_start(type_i[:, :], etype).then_inc(loaded, 16)
                sp.wait_ge(rel_zeroed, 1)
                sp.dma_start(rel_in[0:NREL, :], rel_w).then_inc(loaded, 16)

            @block.gpsimd
            def _(pool):
                nc.gpsimd.memset(rel_in[:, :], 0.0).then_inc(rel_zeroed, 1)
                nc.gpsimd.memset(k["S"][:, :], 0.0).then_inc(s_zeroed, 1)
                with pool.Fori(0, NT) as n:
                    lo, hi, off = window(pool, k["table"], n)
                    with pool.Fori(lo, hi) as i:
                        for b in range(U):
                            gather_turn(nc, pool, idx, k["src_id"], rows, key_table, edge_tile(nc, off, i, b), b, i * U + b,
                                        rows_free, free_seen, idx_set, idx_seen, gathered)

            @block.vector
            def _(dve):
                dve.sem_inc(rows_free, U)
                dve.sem_inc(multiplied, U)
                dve.wait_ge(loaded, 32)
                nc.vector.tensor_copy(typef[:, :], type_i[:, :]).then_inc(rel_ready, 1)
                nc.vector.tensor_scalar(rel_sb[:, :, :], rel_in[:, :].rearrange("p (a d) -> p a d", a=1).to_broadcast([P, H, HD]), 0.2, None, ALU.mult).then_inc(rel_ready, 1)
                dve.wait_ge(s_zeroed, 1)
                dve.wait_ge(rel_ready, 2)
                with dve.Fori(0, NT) as n:
                    lo, hi, off = window(dve, k["table"], n)
                    nc.vector.tensor_scalar(cols[:, :], k["node_col"][:, :], k["tile_base"][:, bass.ds(n, 1)], None, ALU.add).then_inc(cols_set, 1)
                    dve.wait_ge(cols_set, n + 1)
                    dve.sem_inc(cols_seen, 1)
                    with dve.Fori(lo, hi) as i:
                        for b in range(U):
                            t = edge_tile(nc, off, i, b)
                            dve.wait_ge(turned, i * U + b + 1)
                            nc.vector.tensor_scalar(pick[:, b, 0, :], cols[:, :], k["dstf"][:, bass.ds(t, 1)], None, ALU.is_equal)
                            nc.vector.tensor_scalar(pick[:, b, 1, :], k["node_col"][:, :], typef[:, bass.ds(t, 1)], None, ALU.is_equal).then_inc(picked, 1)
                        for b in range(U):
                            dve.wait_ge(gathered[b], i * 16 + 16)
                            dve.wait_ge(made, i * U + b + 1)
                            nc.vector.tensor_tensor(key[:, b, :], ps_q[b][:, D:2 * D], rows[:, b, :], ALU.add).then_inc(rows_free, 1)
                        for b in range(U):
                            dve.wait_ge(rows_free, i * U + b + 1 + U)
                            nc.vector.tensor_tensor(prod[:, b, :], ps_q[b][:, 0:D], key[:, b, :], ALU.mult).then_inc(multiplied, 1)
                        for b in range(U):
                            dve.wait_ge(multiplied, i * U + b + 1 + U)
                            nc.vector.tensor_reduce(score[:, b, :], prod[:, b, :].rearrange("p (h d) -> p h d", h=H), AX.X, ALU.add).then_inc(reduced, 1)
                        dve.wait_ge(reduced, i * U + U)
                        s_t = k["S"][:, bass.ds(edge_tile(nc, off, i, 0) * H, U * H)]
                        nc.vector.tensor_tensor(s_t, s_t, score[:, :, :].rearrange("p b h -> p (b h)"), ALU.add).then_inc(score_added, 1)
                        dve.wait_ge(score_added, i + 1)
                        dve.sem_inc(cols_seen, 1)
                    dve.wait_ge(picked, hi * U)
                    dve.sem_inc(cols_seen, 1)

            @block.scalar
            def _(act):
                with act.Fori(0, NT) as n:
                    lo, hi, off = window(act, k["table"], n)
                    with act.Fori(lo, hi) as i:
                        for b in range(U):
                            act.wait_ge(turned, i * U + b + 1 + U)
                            nc.scalar.copy(pick_T[:, b, :, :].rearrange("p a e -> p (a e)"), ps_t[b % 2][:, 0:2 * P]).then_inc(pick_T_ready, 1)

            @block.tensor
            def _(pe):
                pe.sem_inc(turned, U)
                pe.wait_ge(rel_ready, 2)
                with pe.Fori(0, NT) as n:
                    lo, hi, off = window(pe, k["table"], n)
                    with pe.Fori(lo, hi) as i:
                        def turn(b):
                            pe.wait_ge(picked, i * U + b + 1)
                            for a in range(2):
                                ins = nc.tensor.transpose(ps_t[b % 2][:, a * P:(a + 1) * P], pick[:, b, a, :], k["ident"][:, :])
                            ins.then_inc(turned, 1)
                        turn(0)
                        for b in range(U):
                            if b + 1 < U:
                                turn(b + 1)
                            pe.wait_ge(multiplied, i * U + b + 1)
                            pe.wait_ge(pick_T_ready, i * U + b + 1)
                            nc.tensor.matmul(ps_q[b][:, 0:D], pick_T[:, b, 0, :], k["NODE2"][:, bass.ds(n, 1), :].rearrange("p a d -> p (a d)"), start=True, stop=True)
                            nc.tensor.matmul(ps_q[b][:, D:2 * D], pick_T[:, b, 1, :], rel_sb[:, :, :].rearrange("p h d -> p (h d)"), start=True, stop=True).then_inc(made, 1)


def greatest_scores(nc, k, dst_flat, score_rows):
    with Phase(nc, "gs") as phase:
        sb, ps, sem = phase.sb, phase.ps, phase.sem
        SC = ET * H
        CH = -(-SC // P)
        turned_rows = sb("turned_rows", [P, 2, P])
        V = 2
        HU = U // V
        sc = sb("sc", [P, V, HU * H * P])
        dr = sb("dr", [P, V, HU * P], I32)
        outside = sb("outside", [P, V, HU, P])
        masked = sb("masked", [P, H, HU, P])
        part = sb("part", [P, V, H])
        ps_t = [ps(f"ps_t{b}") for b in range(2)]
        turned, copied, stored, rows_there = (sem(n) for n in ("turned", "copied", "stored", "rows_there"))
        loaded = [sem(f"loaded{v}") for v in range(V)]
        half_done, marked, best_set, best_seen = (sem(n) for n in ("half_done", "marked", "best_set", "best_seen"))
        with nc.Block() as block:
            @block.tensor
            def _(pe):
                for c in range(CH):
                    w = min(P, SC - c * P)
                    if c >= 2:
                        pe.wait_ge(copied, c - 1)
                    nc.tensor.transpose(ps_t[c % 2][0:w, 0:P], k["S"][:, c * P:c * P + w], k["ident"][:, :]).then_inc(turned, 1)

            @block.scalar
            def _(act):
                for c in range(CH):
                    w = min(P, SC - c * P)
                    act.wait_ge(turned, c + 1)
                    if c >= 2:
                        act.wait_ge(stored, 16 * (c - 1))
                    nc.scalar.copy(turned_rows[0:w, c % 2, :], ps_t[c % 2][0:w, 0:P]).then_inc(copied, 1)

            @block.sync
            def _(sp):
                for c in range(CH):
                    w = min(P, SC - c * P)
                    sp.wait_ge(copied, c + 1)
                    if c:
                        sp.wait_ge(stored, 16 * c)
                    sp.dma_start(score_rows[c * P:c * P + w, :], turned_rows[0:w, c % 2, :]).then_inc(stored, 16)
                sp.wait_ge(stored, 16 * CH)
                with sp.Fori(0, NT) as n:
                    lo, hi, off = window(sp, k["table"], n)
                    with sp.Fori(lo, hi) as i:
                        for v in range(V):
                            t = edge_tile(nc, off, i, v * HU)
                            sp.wait_ge(half_done, i * V + v + 1)
                            sp.dma_start(sc[:, v, :], score_rows[bass.ds(t * H, HU * H), :].rearrange("(a t) e -> a (t e)", a=1).to_broadcast([P, HU * H * P])).then_inc(loaded[v], 16)
                            sp.dma_start(dr[:, v, :], dst_flat[bass.ds(t, HU), :].rearrange("(a t) e -> a (t e)", a=1).to_broadcast([P, HU * P])).then_inc(loaded[v], 16)

            @block.vector
            def _(dve):
                dve.sem_inc(half_done, V)
                nc.vector.memset(k["M"][:, :], NEG).then_inc(best_set, 1)
                dve.wait_ge(best_set, 1)
                with dve.Fori(0, NT) as n:
                    lo, hi, off = window(dve, k["table"], n)
                    with dve.Fori(lo, hi) as i:
                        for v in range(V):
                            dve.wait_ge(loaded[v], i * 32 + 32)
                            nc.vector.tensor_scalar(outside[:, v, :, :].rearrange("p t e -> p (t e)"), dr[:, v, :], k["node_id"][:, bass.ds(n, 1)], NEG,
                                                    ALU.not_equal, ALU.mult).then_inc(marked, 1)
                            dve.wait_ge(marked, i * V + v + 1)
                            dve.sem_inc(best_seen, 1)
                            for h in range(H):
                                ins = nc.vector.tensor_tensor_reduce(
                                    out=masked[:, h, :, :], in0=sc[:, v, :].rearrange("p (t h e) -> p h t e", t=HU, h=H)[:, h, :, :],
                                    in1=outside[:, v, :, :], scale=1.0, scalar=NEG, op0=ALU.add, op1=ALU.max, accum_out=part[:, v, h:h + 1])
                            ins.then_inc(half_done, 1)
                            dve.wait_ge(half_done, i * V + v + 1 + V)
                            m = k["M"][:, bass.ds(n * H, H)]
                            nc.vector.tensor_tensor(m, m, part[:, v, :], ALU.max).then_inc(best_set, 1)
                            dve.wait_ge(best_set, i * V + v + 2)
                            dve.sem_inc(best_seen, 1)


def attention_edges(nc, k, value_table):
    with Phase(nc, "ae") as phase:
        sb, ps, sem = phase.sb, phase.ps, phase.sem
        idx = sb("idx", [P, U], I32)
        rows = sb("rows", [P, U, D])
        pick = sb("pick", [P, U, P])
        pick_T = sb("pick_T", [P, U, P])
        low = sb("low", [P, U, H])
        diff = sb("diff", [P, U, H])
        weighted = sb("weighted", [P, U, D + H])
        cols = sb("cols", [P, P])
        acc = ps("acc")
        ps_t = [ps("ps_t0"), ps("ps_t1")]
        ps_m = [ps(f"ps_m{b}") for b in range(U)]
        gathered = [sem(f"gathered{b}") for b in range(U)]
        idx_set, idx_seen, rows_free, free_seen = (sem(n) for n in ("idx_set", "idx_seen", "rows_free", "free_seen"))
        cols_set, cols_seen, picked, turned, pick_T_ready, made = (sem(n) for n in ("cols_set", "cols_seen", "picked", "turned", "pick_T_ready", "made"))
        lowered, subtracted, raised, summed, acc_done, acc_free = (sem(n) for n in ("lowered", "subtracted", "raised", "summed", "acc_done", "acc_free"))
        with nc.Block() as block:
            @block.gpsimd
            def _(pool):
                with pool.Fori(0, NT) as n:
                    lo, hi, off = window(pool, k["table"], n)
                    with pool.Fori(lo, hi) as i:
                        for b in range(U):
                            gather_turn(nc, pool, idx, k["src_id"], rows, value_table, edge_tile(nc, off, i, b), b, i * U + b,
                                        rows_free, free_seen, idx_set, idx_seen, gathered)

            @block.vector
            def _(dve):
                dve.sem_inc(rows_free, U)
                dve.sem_inc(subtracted, U)
                with dve.Fori(0, NT) as n:
                    lo, hi, off = window(dve, k["table"], n)
                    nc.vector.tensor_scalar(cols[:, :], k["node_col"][:, :], k["tile_base"][:, bass.ds(n, 1)], None, ALU.add).then_inc(cols_set, 1)
                    dve.wait_ge(cols_set, n + 1)
                    dve.sem_inc(cols_seen, 1)
                    with dve.Fori(lo, hi) as i:
                        for b in range(U):
                            dve.wait_ge(summed, i * U + b + 1)
                            nc.vector.tensor_scalar(pick[:, b, :], cols[:, :], k["dstf"][:, bass.ds(edge_tile(nc, off, i, b), 1)], None,
                                                    ALU.is_equal).then_inc(picked, 1)
                        for b in range(U):
                            dve.wait_ge(made, i * U + b + 1)
                            nc.vector.tensor_tensor(low[:, b, :], ps_m[b][:, 0:H], k["S"][:, bass.ds(edge_tile(nc, off, i, b) * H, H)], ALU.min).then_inc(lowered, 1)
                        for b in range(U):
                            dve.wait_ge(lowered, i * U + b + 1)
                            nc.vector.tensor_tensor(diff[:, b, :], low[:, b, :], ps_m[b][:, 0:H], ALU.subtract).then_inc(subtracted, 1)
                        for b in range(U):
                            dve.wait_ge(gathered[b], i * 16 + 16)
                            dve.wait_ge(raised, i * U + b + 1)
                            nc.vector.tensor_tensor(weighted[:, b, 0:D].rearrange("p (h d) -> p h d", h=H), rows[:, b, :].rearrange("p (h d) -> p h d", h=H),
                                                    weighted[:, b, D:D + H].rearrange("p (h a) -> p h a", a=1).to_broadcast([P, H, HD]), ALU.mult).then_inc(rows_free, 1)
                    dve.wait_ge(picked, hi * U)
                    dve.sem_inc(cols_seen, 1)

            @block.scalar
            def _(act):
                act.sem_inc(acc_free, 1)
                with act.Fori(0, NT) as n:
                    lo, hi, off = window(act, k["table"], n)
                    with act.Fori(lo, hi) as i:
                        for b in range(U):
                            act.wait_ge(turned, i * U + b + 1)
                            nc.scalar.copy(pick_T[:, b, :], ps_t[b % 2][:, 0:P]).then_inc(pick_T_ready, 1)
                        for b in range(U):
                            act.wait_ge(summed, i * U + b + 1)
                            act.wait_ge(subtracted, i * U + b + 1 + U)
                            nc.scalar.activation(weighted[:, b, D:D + H], diff[:, b, :], ACT.Exp).then_inc(raised, 1)
                    act.wait_ge(acc_done, n + 1)
                    nc.scalar.copy(k["AGG"][:, bass.ds(n, 1), :].rearrange("p a d -> p (a d)"), acc[:, 0:AW]).then_inc(acc_free, 1)

            @block.tensor
            def _(pe):
                pe.sem_inc(summed, U)
                with pe.Fori(0, NT) as n:
                    lo, hi, off = window(pe, k["table"], n)
                    pe.wait_ge(acc_free, n + 1)
                    nc.tensor.matmul(acc[:, 0:AW], k["zeros"][0:1, 0:P], k["zeros"][0:1, 0:AW], start=True, stop=False)
                    with pe.Fori(lo, hi) as i:
                        def turn(b):
                            pe.wait_ge(picked, i * U + b + 1)
                            nc.tensor.transpose(ps_t[b % 2][:, 0:P], pick[:, b, :], k["ident"][:, :]).then_inc(turned, 1)
                        turn(0)
                        for b in range(U):
                            if b + 1 < U:
                                turn(b + 1)
                            pe.wait_ge(subtracted, i * U + b + 1)
                            pe.wait_ge(pick_T_ready, i * U + b + 1)
                            nc.tensor.matmul(ps_m[b][:, 0:H], pick_T[:, b, :], k["M"][:, bass.ds(n * H, H)], start=True, stop=True).then_inc(made, 1)
                        for b in range(U):
                            pe.wait_ge(rows_free, i * U + b + 1 + U)
                            nc.tensor.matmul(acc[:, 0:AW], pick[:, b, :], weighted[:, b, :], start=False, stop=False).then_inc(summed, 1)
                    nc.tensor.matmul(acc[:, 0:AW], k["zeros"][0:1, 0:P], k["zeros"][0:1, 0:AW], start=False, stop=True).then_inc(acc_done, 1)


def tensor_product_edges(nc, k, y, ea10, w_mlp1, w_mlp2, src_table):
    with Phase(nc, "te") as phase:
        sb, ps, sem = phase.sb, phase.ps, phase.sem
        y_sb = k["S"][:, :].rearrange("p (t c) -> p t c", c=4)
        W1 = sb("W1", [NB, NHID])
        W2_in = sb("W2_in", [NHID, D])
        W2 = sb("W2", [NHID, D])
        idx = sb("idx", [P, U], I32)
        y_now = sb("y_now", [P, U, 4])
        rows = sb("rows", [P, U, D])
        edge_T = sb("edge_T", [NB, U, P])
        hid_T = sb("hid_T", [NHID, U, P])
        pick = sb("pick", [P, U, P])
        g_y0 = sb("g_y0", [P, U, D])
        g1_y = sb("g1_y", [P, U, 3, MUL])
        dot = sb("dot", [P, U, MUL])
        wc_g0 = sb("wc_g0", [P, U, MUL])
        msg = sb("msg", [P, U, 512])
        cols = sb("cols", [P, P])
        acc = ps("acc")
        ps_h = [ps("ps_h0"), ps("ps_h1")]
        ps_w = [ps(f"ps_w{b}") for b in range(U)]
        w_loaded, w_ready = sem("w_loaded"), sem("w_ready")
        gathered = [sem(f"gathered{b}") for b in range(U)]
        loaded = [sem(f"loaded{b}") for b in range(U)]
        idx_set, idx_seen, rows_free, free_seen, y_set, y_seen = (sem(n) for n in ("idx_set", "idx_seen", "rows_free", "free_seen", "y_set", "y_seen"))
        cols_set, cols_seen, picked, made, hidden, hid_ready = (sem(n) for n in ("cols_set", "cols_seen", "picked", "made", "hidden", "hid_ready"))
        scaled, crossed, dotted, wc_ready, msg_ready, summed, acc_done, acc_free = (
            sem(n) for n in ("scaled", "crossed", "dotted", "wc_ready", "msg_ready", "summed", "acc_done", "acc_free"))
        with nc.Block() as block:
            @block.sync
            def _(sp):
                sp.dma_start(y_sb[:, :, :], y).then_inc(w_loaded, 16)
                sp.dma_start(W1[:, :], w_mlp1).then_inc(w_loaded, 16)
                sp.dma_start(W2_in[:, :], w_mlp2).then_inc(w_loaded, 16)
                with sp.Fori(0, NT) as n:
                    lo, hi, off = window(sp, k["table"], n)
                    with sp.Fori(lo, hi) as i:
                        for b in range(U):
                            sp.wait_ge(hidden, i * U + b + 1)
                            sp.dma_start(edge_T[:, b, :], ea10[bass.ds(edge_tile(nc, off, i, b), 1), :, :].rearrange("a p e -> (a p) e")).then_inc(loaded[b], 16)

            @block.gpsimd
            def _(pool):
                pool.wait_ge(w_ready, 2)
                with pool.Fori(0, NT) as n:
                    lo, hi, off = window(pool, k["table"], n)
                    with pool.Fori(lo, hi) as i:
                        for b in range(U):
                            pool.wait_ge(summed, i * U + b + 1)
                            pool.sem_inc(y_seen, 1)
                            nc.gpsimd.tensor_copy(y_now[:, b, :], y_sb[:, bass.ds(edge_tile(nc, off, i, b), 1), :].rearrange("p a c -> p (a c)")).then_inc(y_set, 1)
                            gather_turn(nc, pool, idx, k["src_id"], rows, src_table, edge_tile(nc, off, i, b), b, i * U + b,
                                        rows_free, free_seen, idx_set, idx_seen, gathered)

            @block.vector
            def _(dve):
                dve.sem_inc(rows_free, U)
                dve.wait_ge(w_loaded, 48)
                for a in range(4):
                    nc.vector.tensor_scalar(W2[:, a * MUL:(a + 1) * MUL], W2_in[:, a * MUL:(a + 1) * MUL], float(NHID ** -0.5 * (3 ** -0.5 if a == 1 else 1.0)), None,
                                            ALU.mult).then_inc(w_ready, 1)
                with dve.Fori(0, NT) as n:
                    lo, hi, off = window(dve, k["table"], n)
                    nc.vector.tensor_scalar(cols[:, :], k["node_col"][:, :], k["tile_base"][:, bass.ds(n, 1)], None, ALU.add).then_inc(cols_set, 1)
                    dve.wait_ge(cols_set, n + 1)
                    dve.sem_inc(cols_seen, 1)
                    with dve.Fori(lo, hi) as i:
                        for b in range(U):
                            s = i * U + b
                            dve.wait_ge(summed, s + 1)
                            nc.vector.tensor_scalar(pick[:, b, :], cols[:, :], k["dstf"][:, bass.ds(edge_tile(nc, off, i, b), 1)], None,
                                                    ALU.is_equal).then_inc(picked, 1)
                            dve.wait_ge(y_set, s + 1)
                            dve.wait_ge(gathered[b], i * 16 + 16)
                            nc.vector.tensor_tensor(g1_y[:, b, :, :], rows[:, b, MUL:D].rearrange("p (m u) -> p m u", m=3),
                                                    y_now[:, b, 1:4].rearrange("p (m a) -> p m a", a=1).to_broadcast([P, 3, MUL]), ALU.mult).then_inc(crossed, 1)
                            dve.wait_ge(made, s + 1)
                            nc.vector.tensor_tensor(wc_g0[:, b, :], ps_w[b][:, 2 * MUL:3 * MUL], rows[:, b, 0:MUL], ALU.mult).then_inc(rows_free, 1)
                            dve.wait_ge(crossed, s + 1)
                            nc.vector.tensor_reduce(dot[:, b, :], g1_y[:, b, :, :].rearrange("p m u -> p u m"), AX.X, ALU.add).then_inc(dotted, 1)
                            dve.wait_ge(scaled, s + 1)
                            nc.vector.tensor_tensor(msg[:, b, 0:MUL], ps_w[b][:, 0:MUL], g_y0[:, b, 0:MUL], ALU.mult)
                            vec = msg[:, b, 2 * MUL:8 * MUL].rearrange("p (m a u) -> p m a u", m=3, a=2)
                            nc.vector.tensor_tensor(vec[:, :, 1, :], g_y0[:, b, MUL:D].rearrange("p (m u) -> p m u", m=3),
                                                    ps_w[b][:, 3 * MUL:4 * MUL].rearrange("p (a u) -> p a u", a=1).to_broadcast([P, 3, MUL]), ALU.mult)
                            dve.wait_ge(rows_free, s + 1 + U)
                            nc.vector.tensor_tensor(vec[:, :, 0, :], wc_g0[:, b, :].rearrange("p (a u) -> p a u", a=1).to_broadcast([P, 3, MUL]),
                                                    y_now[:, b, 1:4].rearrange("p (m a) -> p m a", a=1).to_broadcast([P, 3, MUL]), ALU.mult)
                            dve.wait_ge(dotted, s + 1)
                            nc.vector.tensor_tensor(msg[:, b, MUL:2 * MUL], ps_w[b][:, MUL:2 * MUL], dot[:, b, :], ALU.mult).then_inc(msg_ready, 1)
                    dve.wait_ge(picked, hi * U)
                    dve.sem_inc(cols_seen, 1)

            @block.scalar
            def _(act):
                act.sem_inc(acc_free, 1)
                with act.Fori(0, NT) as n:
                    lo, hi, off = window(act, k["table"], n)
                    with act.Fori(lo, hi) as i:
                        for b in range(U):
                            s = i * U + b
                            act.wait_ge(hidden, s + 1 + U)
                            nc.scalar.activation(hid_T[:, b, :], ps_h[b % 2][0:NHID, 0:P], ACT.Silu, scale=float(NB ** -0.5)).then_inc(hid_ready, 1)
                            act.wait_ge(summed, s + 1)
                            act.wait_ge(y_set, s + 1)
                            act.wait_ge(gathered[b], i * 16 + 16)
                            nc.scalar.activation(g_y0[:, b, :], rows[:, b, :], ACT.Copy, scale=y_now[:, b, 0:1]).then_inc(scaled, 1)
                    act.wait_ge(acc_done, n + 1)
                    nc.scalar.copy(k["AGG2"][:, bass.ds(n, 1), :].rearrange("p a d -> p (a d)"), acc[:, :]).then_inc(acc_free, 1)

            @block.tensor
            def _(pe):
                pe.sem_inc(summed, U)
                pe.sem_inc(hidden, U)
                pe.wait_ge(w_ready, 4)
                with pe.Fori(0, NT) as n:
                    lo, hi, off = window(pe, k["table"], n)
                    pe.wait_ge(acc_free, n + 1)
                    nc.tensor.matmul(acc[:, :], k["zeros"][0:1, 0:P], k["zeros"][0:1, :], start=True, stop=False)
                    with pe.Fori(lo, hi) as i:
                        def hide(b):
                            pe.wait_ge(loaded[b], i * 16 + 16)
                            nc.tensor.matmul(ps_h[b % 2][0:NHID, 0:P], W1[:, :], edge_T[:, b, :], start=True, stop=True).then_inc(hidden, 1)

                        def add_up(b):
                            pe.wait_ge(msg_ready, i * U + b + 1)
                            nc.tensor.matmul(acc[:, :], pick[:, b, :], msg[:, b, :], start=False, stop=False).then_inc(summed, 1)
                        hide(0)
                        for b in range(U):
                            if b + 1 < U:
                                hide(b + 1)
                            pe.wait_ge(hid_ready, i * U + b + 1)
                            nc.tensor.matmul(ps_w[b][:, 0:D], hid_T[:, b, :], W2[:, :], start=True, stop=True).then_inc(made, 1)
                            if b:
                                add_up(b - 1)
                        add_up(U - 1)
                    nc.tensor.matmul(acc[:, :], k["zeros"][0:1, 0:P], k["zeros"][0:1, :], start=False, stop=True).then_inc(acc_done, 1)


def flat(ap):
    return ap.rearrange("p a d -> p (a d)")


def statistics(nc, dve, step, tiles, stats, mean_var, std_wanted, std_ready, turn, rstd):
    for j, tile in enumerate(tiles):
        ins = nc.vector.bn_stats(stats[:, j, :], tile)
    step.then_wait(ins)
    dve.sem_inc(std_wanted[1], 1)
    for j in range(GN):
        ins = nc.vector.bn_aggr(mean_var[:, j, :], stats[:, j, :])
    step.then_wait(ins)
    dve.sem_inc(std_wanted[1], 1)
    nc.vector.tensor_scalar(rstd[:, :], mean_var[:, :, 1], 1e-5, None, ALU.add).then_inc(std_wanted[0], 1)
    dve.wait_ge(std_ready, turn + 1)
    step.then_wait(nc.vector.reciprocal(rstd[:, :], rstd[:, :]))
    dve.sem_inc(std_wanted[1], 1)


def normalise_and_project(nc, k, name, add_x, between, load_weights, banks, evacuate, tables):
    with Phase(nc, name) as phase:
        sb, ps, sem = phase.sb, phase.ps, phase.sem
        stats, mean_var, rstd = sb("stats", [P, GN, 6]), sb("mean_var", [P, GN, 2]), sb("rstd", [P, GN])
        z = sb("z", [P, 2, D])
        zin = sb("zin", [P, 2, D]) if between else z
        z_T = sb("z_T", [P, 2, 2, P])
        stage = sb("stage", [P, 2, 512])
        ps_t = [ps(f"ps_t{b}") for b in range(2)]
        ps_a = [ps(f"ps_a{b}") for b in range(2)]
        ps_b = [ps(f"ps_b{b}") for b in range(2)]
        w_loaded, w_ready, stored, zeroed = sem("w_loaded"), sem("w_ready"), sem("stored"), sem("zeroed")
        dve_step, added, std_wanted, seen, std_ready, z_ready = (
            sem(n) for n in ("dve_step", "added", "std_wanted", "seen", "std_ready", "z_ready"))
        x_put, zin_ready, turned, z_T_ready, made, staged, stage_free, pool_seen = (
            sem(n) for n in ("x_put", "zin_ready", "turned", "z_T_ready", "made", "staged", "stage_free", "pool_seen"))
        W = load_weights(sb)
        STEPS = 3
        with nc.Block() as block:
            @block.sync
            def _(sp):
                if W.get("zeroed"):
                    sp.wait_ge(zeroed, len(W["zeroed"]))
                for dst, src in W["loads"]:
                    sp.dma_start(dst, src).then_inc(w_loaded, 16)
                sp.sem_inc(stage_free, LAG)
                with sp.Fori(0, NG) as g:
                    for j in range(GN):
                        b, _ = buffer_of(j)
                        s = g * GN + j
                        sp.wait_ge(staged, s + 1 + LAG)
                        for table, c0, c1 in tables:
                            sp.dma_start(table[bass.ds(s * P, P), :], stage[:, b, c0:c1]).then_inc(stored, 16)
                        sp.wait_ge(stored, (s + 1) * 16 * len(tables))
                        sp.sem_inc(stage_free, 1)

            @block.gpsimd
            def _(pool):
                for dst in W.get("zeroed", ()):
                    nc.gpsimd.memset(dst, 0.0).then_inc(zeroed, 1)
                if W["ready"]:
                    pool.wait_ge(w_ready, W["ready"])
                with pool.Fori(0, NG) as g:
                    for j in range(GN):
                        b, back = buffer_of(j)
                        s = g * GN + j
                        pool.wait_ge(z_ready, s + 1)
                        pool.sem_inc(pool_seen, 1)
                        nc.gpsimd.tensor_copy(flat(k["X"][:, bass.ds(s, 1), :]), z[:, b, :]).then_inc(x_put, 1)
                        if between:
                            pool.wait_ge(turned, s - back + 1 + LAG)
                            pool.sem_inc(pool_seen, 1)
                            between(nc, W, zin[:, b, :], z[:, b, :]).then_inc(zin_ready, 1)

            @block.vector
            def _(dve):
                dve.sem_inc(staged, LAG)
                dve.wait_ge(w_loaded, 16 * len(W["loads"]))
                W["prepare"](nc, dve, w_ready)
                if W["ready"]:
                    dve.wait_ge(w_ready, W["ready"])
                    dve.sem_inc(seen, 1)
                with dve.Fori(0, NG) as g:
                    step = Count(dve, dve_step, g, STEPS)
                    if add_x:
                        agg = k["AGG"][:, bass.ds(g * GN, GN), 0:D]
                        nc.vector.tensor_tensor(agg, agg, k["X"][:, bass.ds(g * GN, GN), :], ALU.add).then_inc(added, 1)
                        dve.wait_ge(added, g + 1)
                        dve.sem_inc(seen, 1)
                    statistics(nc, dve, step, [flat(k["AGG"][:, bass.ds(g * GN + j, 1), 0:D]) for j in range(GN)], stats, mean_var,
                               (std_wanted, seen), std_ready, g, rstd)
                    step.full()

                    def normalise(j):
                        b, back = buffer_of(j)
                        s = g * GN + j
                        dve.wait_ge(x_put, s - back + 1 + LAG)
                        dve.wait_ge(zin_ready if between else turned, s - back + 1 + LAG)
                        nc.vector.tensor_scalar(z[:, b, :], flat(k["AGG"][:, bass.ds(s, 1), 0:D]), mean_var[:, j, 0:1], rstd[:, j:j + 1],
                                                ALU.subtract, ALU.mult).then_inc(z_ready, 1)

                    def take(j):
                        b, back = buffer_of(j)
                        s = g * GN + j
                        dve.wait_ge(stage_free, s - back + 1 + LAG)
                        dve.wait_ge(made, s + 1)
                        evacuate(nc, k, W, s, ps_a[b], ps_b[b], stage[:, b, :]).then_inc(staged, 1)
                    normalise(0)
                    for j in range(GN):
                        if j + 1 < GN:
                            normalise(j + 1)
                        take(j)

            @block.scalar
            def _(act):
                act.sem_inc(x_put, LAG)
                act.sem_inc(zin_ready, LAG)
                with act.Fori(0, NG) as g:
                    act.wait_ge(std_wanted, g + 1)
                    nc.scalar.activation(rstd[:, :], rstd[:, :], ACT.Sqrt).then_inc(std_ready, 1)
                    for j in range(GN):
                        b, back = buffer_of(j)
                        s = g * GN + j
                        act.wait_ge(turned, s + 1 + LAG)
                        nc.scalar.copy(z_T[:, b, :, :].rearrange("p c n -> p (c n)"), ps_t[b][:, 0:2 * P]).then_inc(z_T_ready, 1)

            @block.tensor
            def _(pe):
                pe.sem_inc(turned, LAG)
                pe.wait_ge(w_loaded, 16 * len(W["loads"]))
                if W["ready"]:
                    pe.wait_ge(w_ready, W["ready"])
                with pe.Fori(0, NG) as g:
                    def turn(j):
                        b, back = buffer_of(j)
                        pe.wait_ge(zin_ready if between else z_ready, g * GN + j + 1 + (LAG if between else 0))
                        for c in range(2):
                            ins = nc.tensor.transpose(ps_t[b][:, c * P:(c + 1) * P], zin[:, b, c * P:(c + 1) * P], k["ident"][:, :])
                        ins.then_inc(turned, 1)
                    turn(0)
                    for j in range(GN):
                        b, back = buffer_of(j)
                        s = g * GN + j
                        if j + 1 < GN:
                            turn(j + 1)
                        pe.wait_ge(z_T_ready, s + 1)
                        pe.wait_ge(staged, s - back + 1 + LAG)
                        for bank, c0, c1, terms in banks(W):
                            out = (ps_a, ps_b)[bank][b][:, c0:c1]
                            for m, (c, w) in enumerate(terms):
                                ins = nc.tensor.matmul(out, z_T[:, b, c, :], w, start=(m == 0), stop=(m == len(terms) - 1))
                        ins.then_inc(made, 1)


def spread(vector):
    return vector.rearrange("(a d) -> a d", a=1).to_broadcast([P, vector.shape[0]])


def message_tables(nc, k, w_msg, b_msg, src_table):
    def load_weights(sb):
        w, bias = sb("w", [P, 2, 2 * D]), sb("bias", [P, D])
        return dict(w=w, bias=bias, ready=0, prepare=lambda *_: None, loads=[
            (w[:, :, 0:D], w_msg[0:D, :].rearrange("(c p) o -> p c o", p=P)),
            (w[:, :, D:2 * D], w_msg[D:2 * D, :].rearrange("(c p) o -> p c o", p=P)), (bias[:, :], spread(b_msg))])

    def evacuate(nc, k, W, s, ps_a, ps_b, stage):
        nc.vector.tensor_tensor(stage[:, 0:D], ps_a[:, 0:D], W["bias"][:, :], ALU.add)
        return nc.vector.tensor_copy(flat(k["NODE2"][:, bass.ds(s, 1), :]), ps_a[:, D:2 * D])

    normalise_and_project(nc, k, "mt", True, None, load_weights,
                          lambda W: [(0, 0, 2 * D, [(c, W["w"][:, c, :]) for c in range(2)])], evacuate, [(src_table, 0, D)])


def attention_tables(nc, k, q_emb, wq, bq, wk, bk, wv, bv, key_table, value_table):
    def load_weights(sb):
        w, bias, query = sb("w", [P, 2, 3 * D]), sb("bias", [P, 3 * D]), sb("query", [P, D])

        def prepare(nc, dve, w_ready):
            nc.vector.tensor_scalar(w[:, :, 0:D], w[:, :, 0:D], float(HD ** -0.5), None, ALU.mult).then_inc(w_ready, 1)
            nc.vector.tensor_scalar(bias[:, 0:D], bias[:, 0:D], float(HD ** -0.5), None, ALU.mult).then_inc(w_ready, 1)
            nc.vector.tensor_scalar(query[:, :], query[:, :], 0.1, None, ALU.mult).then_inc(w_ready, 1)
        loads = [(query[:, :], spread(q_emb))]
        for n, (wn, bn) in enumerate(((wq, bq), (wk, bk), (wv, bv))):
            loads += [(w[:, :, n * D:(n + 1) * D], wn.rearrange("(c p) o -> p c o", p=P)), (bias[:, n * D:(n + 1) * D], spread(bn))]
        return dict(w=w, bias=bias, query=query, ready=3, prepare=prepare, loads=loads)

    def between(nc, W, zin, z):
        return nc.gpsimd.tensor_tensor(zin, z, W["query"][:, :], ALU.add)

    def evacuate(nc, k, W, s, ps_a, ps_b, stage):
        nc.vector.tensor_tensor(flat(k["NODE2"][:, bass.ds(s, 1), :]), ps_b[:, 0:D], W["bias"][:, 0:D], ALU.add)
        return nc.vector.tensor_tensor(stage, ps_a[:, :], W["bias"][:, D:3 * D], ALU.add)

    normalise_and_project(nc, k, "at", False, between, load_weights,
                          lambda W: [(1, 0, D, [(c, W["w"][:, c, 0:D]) for c in range(2)]),
                                     (0, 0, 2 * D, [(c, W["w"][:, c, D:3 * D]) for c in range(2)])],
                          evacuate, [(key_table, 0, D), (value_table, D, 2 * D)])


def by_component(ap):
    return ap[:, MUL:D].rearrange("p (u m) -> p m u", m=3)


def product_tables(nc, k, node_attr, w_li0, w_li1, src_table):
    def load_weights(sb):
        w, attr, scale = sb("w", [P, 2, P]), sb("attr", [P, NT]), sb("scale", [P, NT])

        def prepare(nc, dve, w_ready):
            nc.vector.scalar_tensor_tensor(scale[:, :], attr[:, :], float(MUL ** -0.5), k["isq"][:, :], ALU.mult, ALU.mult).then_inc(w_ready, 1)
        loads = [(w[0:MUL, 0, 0:MUL], w_li0), (w[MUL:P, 0, MUL:P], w_li1), (w[0:MUL, 1, 0:MUL], w_li1), (w[MUL:P, 1, MUL:P], w_li1),
                 (attr[:, :], node_attr)]
        return dict(w=w, scale=scale, ready=1, prepare=prepare, loads=loads, zeroed=[w[:, :, :]])

    def between(nc, W, zin, z):
        nc.gpsimd.tensor_copy(zin[:, 0:MUL], z[:, 0:MUL])
        return nc.gpsimd.tensor_copy(zin[:, MUL:D].rearrange("p (m u) -> p m u", m=3), by_component(z))

    def evacuate(nc, k, W, s, ps_a, ps_b, stage):
        return nc.vector.tensor_scalar(stage[:, 0:D], ps_a[:, 0:D], W["scale"][:, bass.ds(s, 1)], None, ALU.mult)

    normalise_and_project(nc, k, "pt", False, between, load_weights,
                          lambda W: [(0, 0, P, [(0, W["w"][:, 0, :])]), (0, P, D, [(1, W["w"][:, 1, :])])], evacuate, [(src_table, 0, D)])


def update_nodes(nc, k, w_upd, b_upd):
    with Phase(nc, "u") as phase:
        sb, ps, sem = phase.sb, phase.ps, phase.sem
        W, bias, inv = sb("W", [P, 4, D]), sb("bias", [P, D]), sb("inv", [P, NT])
        xs, ag, both_T, pre = sb("xs", [P, 2, D]), sb("ag", [P, 2, D]), sb("both_T", [P, 2, 4, P]), sb("pre", [P, 2, D])
        ps_t = [ps(f"ps_t{b}") for b in range(2)]
        ps_o = [ps(f"ps_o{b}") for b in range(2)]
        w_loaded, dve_step, seen, xs_ready, ag_ready, turned, both_ready, made, pre_ready, put = (
            sem(n) for n in ("w_loaded", "dve_step", "seen", "xs_ready", "ag_ready", "turned", "both_ready", "made", "pre_ready", "put"))
        with nc.Block() as block:
            @block.sync
            def _(sp):
                sp.dma_start(W[:, :, :], w_upd.rearrange("(c p) o -> p c o", p=P)).then_inc(w_loaded, 16)
                sp.dma_start(bias[:, :], spread(b_upd)).then_inc(w_loaded, 16)

            @block.gpsimd
            def _(pool):
                with pool.Fori(0, NG) as g:
                    for j in range(GN):
                        b, back = buffer_of(j)
                        s = g * GN + j
                        pool.wait_ge(put, s - back + 1 + LAG)
                        pool.sem_inc(seen, 1)
                        nc.gpsimd.tensor_copy(xs[:, b, :], flat(k["X"][:, bass.ds(s, 1), :])).then_inc(xs_ready, 1)

            @block.vector
            def _(dve):
                dve.sem_inc(put, LAG)
                step = Count(dve, dve_step)
                dve.wait_ge(w_loaded, 32)
                step.then_wait(nc.vector.tensor_copy(k["count"][:, :], k["AGG"][:, :, D]))
                step.then_wait(nc.vector.tensor_scalar(inv[:, :], k["count"][:, :], 1e-6, None, ALU.add))
                step.then_wait(nc.vector.reciprocal(inv[:, :], inv[:, :]))
                dve.sem_inc(seen, 1)
                with dve.Fori(0, NG) as g:
                    def mean(j):
                        b, back = buffer_of(j)
                        s = g * GN + j
                        dve.wait_ge(turned, s - back + 1 + LAG)
                        nc.vector.tensor_scalar(ag[:, b, :], flat(k["AGG"][:, bass.ds(s, 1), 0:D]), inv[:, bass.ds(s, 1)], None, ALU.mult).then_inc(ag_ready, 1)
                    mean(0)
                    for j in range(GN):
                        b, back = buffer_of(j)
                        s = g * GN + j
                        if j + 1 < GN:
                            mean(j + 1)
                        dve.wait_ge(made, s + 1)
                        nc.vector.tensor_tensor(pre[:, b, :], ps_o[b][:, 0:D], bias[:, :], ALU.add).then_inc(pre_ready, 1)
                        dve.wait_ge(xs_ready, s + 1)
                        dve.wait_ge(pre_ready, s + 1)
                        dve.sem_inc(seen, 1)
                        nc.vector.scalar_tensor_tensor(flat(k["AGG"][:, bass.ds(s, 1), 0:D]), pre[:, b, :], 0.0, xs[:, b, :], ALU.max, ALU.add).then_inc(put, 1)

            @block.scalar
            def _(act):
                with act.Fori(0, NG) as g:
                    for j in range(GN):
                        b, _ = buffer_of(j)
                        s = g * GN + j
                        act.wait_ge(turned, s + 1 + LAG)
                        nc.scalar.copy(both_T[:, b, :, :].rearrange("p c n -> p (c n)"), ps_t[b][:, :]).then_inc(both_ready, 1)

            @block.tensor
            def _(pe):
                pe.sem_inc(turned, LAG)
                pe.wait_ge(w_loaded, 32)
                with pe.Fori(0, NG) as g:
                    def turn(j):
                        b, _ = buffer_of(j)
                        pe.wait_ge(xs_ready, g * GN + j + 1)
                        pe.wait_ge(ag_ready, g * GN + j + 1)
                        for c in range(4):
                            part = (xs, ag)[c // 2][:, b, (c % 2) * P:(c % 2 + 1) * P]
                            ins = nc.tensor.transpose(ps_t[b][:, c * P:(c + 1) * P], part, k["ident"][:, :])
                        ins.then_inc(turned, 1)
                    turn(0)
                    for j in range(GN):
                        b, back = buffer_of(j)
                        s = g * GN + j
                        if j + 1 < GN:
                            turn(j + 1)
                        pe.wait_ge(both_ready, s + 1)
                        pe.wait_ge(put, s - back + 1 + LAG)
                        for c in range(4):
                            ins = nc.tensor.matmul(ps_o[b][:, 0:D], both_T[:, b, c, :], W[:, c, :], start=(c == 0), stop=(c == 3))
                        ins.then_inc(made, 1)


def attention_out(nc, k, wo, bo, value_table):
    with Phase(nc, "ao") as phase:
        sb, ps, sem = phase.sb, phase.ps, phase.sem
        W, bias, empty, inv = sb("W", [P, 2, D]), sb("bias", [P, D]), sb("empty", [P, NT]), sb("inv", [P, NT, H])
        xb, values, mean, mixed, mixed_T = sb("xb", [P, 2, D]), sb("values", [P, 2, D]), sb("mean", [P, 2, D]), sb("mixed", [P, 2, D]), sb("mixed_T", [P, 2, 2, P])
        ps_t = [ps(f"ps_t{b}") for b in range(2)]
        ps_o = [ps(f"ps_o{b}") for b in range(2)]
        loaded = [sem(f"loaded{b}") for b in range(2)]
        w_loaded, dve_step, seen, xb_ready, mean_ready, mixed_ready, turned, mixed_T_ready, made, put = (
            sem(n) for n in ("w_loaded", "dve_step", "seen", "xb_ready", "mean_ready", "mixed_ready", "turned", "mixed_T_ready", "made", "put"))
        with nc.Block() as block:
            @block.sync
            def _(sp):
                sp.dma_start(W[:, :, :], wo.rearrange("(c p) o -> p c o", p=P)).then_inc(w_loaded, 16)
                sp.dma_start(bias[:, :], spread(bo)).then_inc(w_loaded, 16)
                with sp.Fori(0, NG) as g:
                    for j in range(GN):
                        b, back = buffer_of(j)
                        s = g * GN + j
                        per = (GN + 1 - b) // 2
                        sp.wait_ge(mixed_ready, s - back + 1 + LAG)
                        sp.dma_start(values[:, b, :], value_table[bass.ds(s * P, P), :]).then_inc(loaded[b], 16)

            @block.gpsimd
            def _(pool):
                pool.wait_ge(w_loaded, 32)
                with pool.Fori(0, NG) as g:
                    for j in range(GN):
                        b, back = buffer_of(j)
                        s = g * GN + j
                        pool.wait_ge(put, s - back + 1 + LAG)
                        pool.sem_inc(seen, 1)
                        nc.gpsimd.tensor_tensor(xb[:, b, :], flat(k["X"][:, bass.ds(s, 1), :]), bias[:, :], ALU.add).then_inc(xb_ready, 1)

            @block.vector
            def _(dve):
                dve.sem_inc(put, LAG)
                dve.sem_inc(mixed_ready, LAG)
                step = Count(dve, dve_step)
                step.then_wait(nc.vector.tensor_scalar(empty[:, :], k["count"][:, :], 0.0, None, ALU.is_equal))
                step.then_wait(nc.vector.tensor_tensor(inv[:, :, :], k["AGG"][:, :, D:AW], empty[:, :].rearrange("p (n a) -> p n a", a=1).to_broadcast([P, NT, H]), ALU.add))
                step.then_wait(nc.vector.reciprocal(inv[:, :, :].rearrange("p n h -> p (n h)"), inv[:, :, :].rearrange("p n h -> p (n h)")))
                dve.sem_inc(seen, 1)
                with dve.Fori(0, NG) as g:
                    def mix(j):
                        b, back = buffer_of(j)
                        s = g * GN + j
                        per = (GN + 1 - b) // 2
                        nc.vector.tensor_tensor(mean[:, b, :].rearrange("p (h d) -> p h d", h=H), flat(k["AGG"][:, bass.ds(s, 1), 0:D]).rearrange("p (h d) -> p h d", h=H),
                                                flat(inv[:, bass.ds(s, 1), :]).rearrange("p (h a) -> p h a", a=1).to_broadcast([P, H, HD]), ALU.mult).then_inc(mean_ready, 1)
                        dve.wait_ge(turned, s - back + 1 + LAG)
                        dve.wait_ge(loaded[b], (g * per + j // 2) * 16 + 16)
                        dve.wait_ge(mean_ready, s + 1)
                        dve.sem_inc(seen, 1)
                        nc.vector.scalar_tensor_tensor(mixed[:, b, :], values[:, b, :], empty[:, bass.ds(s, 1)], mean[:, b, :], ALU.mult, ALU.add).then_inc(mixed_ready, 1)
                    mix(0)
                    for j in range(GN):
                        b, back = buffer_of(j)
                        s = g * GN + j
                        if j + 1 < GN:
                            mix(j + 1)
                        dve.wait_ge(xb_ready, s + 1)
                        dve.wait_ge(made, s + 1)
                        nc.vector.tensor_tensor(flat(k["AGG"][:, bass.ds(s, 1), 0:D]), ps_o[b][:, 0:D], xb[:, b, :], ALU.add).then_inc(put, 1)

            @block.scalar
            def _(act):
                with act.Fori(0, NG) as g:
                    for j in range(GN):
                        b, _ = buffer_of(j)
                        s = g * GN + j
                        act.wait_ge(turned, s + 1 + LAG)
                        nc.scalar.copy(mixed_T[:, b, :, :].rearrange("p c n -> p (c n)"), ps_t[b][:, 0:2 * P]).then_inc(mixed_T_ready, 1)

            @block.tensor
            def _(pe):
                pe.sem_inc(turned, LAG)
                pe.wait_ge(w_loaded, 32)
                with pe.Fori(0, NG) as g:
                    def turn(j):
                        b, _ = buffer_of(j)
                        pe.wait_ge(mixed_ready, g * GN + j + 1 + LAG)
                        for c in range(2):
                            ins = nc.tensor.transpose(ps_t[b][:, c * P:(c + 1) * P], mixed[:, b, c * P:(c + 1) * P], k["ident"][:, :])
                        ins.then_inc(turned, 1)
                    turn(0)
                    for j in range(GN):
                        b, back = buffer_of(j)
                        s = g * GN + j
                        if j + 1 < GN:
                            turn(j + 1)
                        pe.wait_ge(mixed_T_ready, s + 1)
                        pe.wait_ge(put, s - back + 1 + LAG)
                        for c in range(2):
                            ins = nc.tensor.matmul(ps_o[b][:, 0:D], mixed_T[:, b, c, :], W[:, c, :], start=(c == 0), stop=(c == 1))
                        ins.then_inc(made, 1)


def affine_norm(nc, k, gamma, beta):
    with Phase(nc, "an") as phase:
        sb, ps, sem = phase.sb, phase.ps, phase.sem
        ga, be = sb("ga", [P, D]), sb("be", [P, D])
        stats, mean_var, rstd = sb("stats", [P, GN, 6]), sb("mean_var", [P, GN, 2]), sb("rstd", [P, GN])
        w_loaded, dve_step, seen, std_wanted, std_ready, deg_ready, root_ready = (
            sem(n) for n in ("w_loaded", "dve_step", "seen", "std_wanted", "std_ready", "deg_ready", "root_ready"))
        STEPS = 7
        with nc.Block() as block:
            @block.sync
            def _(sp):
                sp.dma_start(ga[:, :], spread(gamma)).then_inc(w_loaded, 16)
                sp.dma_start(be[:, :], spread(beta)).then_inc(w_loaded, 16)

            @block.vector
            def _(dve):
                nc.vector.tensor_scalar(k["isq"][:, :], k["count"][:, :], 1.0, None, ALU.max).then_inc(deg_ready, 1)
                dve.wait_ge(root_ready, 1)
                nc.vector.reciprocal(k["isq"][:, :], k["isq"][:, :])
                dve.wait_ge(w_loaded, 32)
                with dve.Fori(0, NG) as g:
                    step = Count(dve, dve_step, g, STEPS)
                    statistics(nc, dve, step, [flat(k["AGG"][:, bass.ds(g * GN + j, 1), 0:D]) for j in range(GN)], stats, mean_var,
                               (std_wanted, seen), std_ready, g, rstd)
                    for j in range(GN):
                        z = flat(k["AGG"][:, bass.ds(g * GN + j, 1), 0:D])
                        ins = nc.vector.tensor_scalar(z, z, mean_var[:, j, 0:1], rstd[:, j:j + 1], ALU.subtract, ALU.mult)
                    step.then_wait(ins)
                    dve.sem_inc(seen, 1)
                    z = k["AGG"][:, bass.ds(g * GN, GN), 0:D]
                    for other, op in ((ga[:, :].rearrange("p (a d) -> p a d", a=1).to_broadcast([P, GN, D]), ALU.mult),
                                      (be[:, :].rearrange("p (a d) -> p a d", a=1).to_broadcast([P, GN, D]), ALU.add),
                                      (k["X"][:, bass.ds(g * GN, GN), :], ALU.add)):
                        step.then_wait(nc.vector.tensor_tensor(z, z, other, op))
                        dve.sem_inc(seen, 1)
                    step.full()

            @block.scalar
            def _(act):
                act.wait_ge(deg_ready, 1)
                nc.scalar.activation(k["isq"][:, :], k["isq"][:, :], ACT.Sqrt).then_inc(root_ready, 1)
                with act.Fori(0, NG) as g:
                    act.wait_ge(std_wanted, g + 1)
                    nc.scalar.activation(rstd[:, :], rstd[:, :], ACT.Sqrt).then_inc(std_ready, 1)


def product_out(nc, k, node_attr, w_lm0, w_lm1, w_lo0, w_lo1):
    import math
    with Phase(nc, "po") as phase:
        sb, ps, sem = phase.sb, phase.ps, phase.sem
        own_in, own, mid_w, attr, scale = sb("own_in", [P, 2, P]), sb("own", [P, 2, P]), sb("mid_w", [P, 2, MUL]), sb("attr", [P, NT]), sb("scale", [P, NT])
        xp, mid, both_T = sb("xp", [P, 2, D]), sb("mid", [P, 2, 512]), sb("both_T", [P, 2, 6, P])
        ps_m = [ps(f"ps_m{b}") for b in range(2)]
        ps_x = [ps(f"ps_x{b}") for b in range(2)]
        ps_o = [ps(f"ps_o{b}") for b in range(2)]
        zeroed, w_loaded, w_ready, seen, xp_ready, mid_ready, turned, both_ready, made, put = (
            sem(n) for n in ("zeroed", "w_loaded", "w_ready", "seen", "xp_ready", "mid_ready", "turned", "both_ready", "made", "put"))
        loads = [(own_in[0:MUL, 0, 0:MUL], w_lm0), (own_in[MUL:P, 0, MUL:P], w_lm1), (own_in[0:MUL, 1, 0:MUL], w_lm1), (own_in[MUL:P, 1, MUL:P], w_lm1),
                 (mid_w[:, 0, :], w_lo0), (mid_w[:, 1, :], w_lo1), (attr[:, :], node_attr)]
        with nc.Block() as block:
            @block.sync
            def _(sp):
                sp.wait_ge(zeroed, 1)
                for dst, src in loads:
                    sp.dma_start(dst, src).then_inc(w_loaded, 16)

            @block.gpsimd
            def _(pool):
                nc.gpsimd.memset(own_in[:, :, :], 0.0).then_inc(zeroed, 1)
                with pool.Fori(0, NG) as g:
                    for j in range(GN):
                        b, back = buffer_of(j)
                        s = g * GN + j
                        x = flat(k["X"][:, bass.ds(s, 1), :])
                        pool.wait_ge(turned, s - back + 1 + LAG)
                        pool.sem_inc(seen, 1)
                        nc.gpsimd.tensor_copy(xp[:, b, 0:MUL], x[:, 0:MUL])
                        nc.gpsimd.tensor_copy(xp[:, b, MUL:D].rearrange("p (m u) -> p m u", m=3), by_component(x)).then_inc(xp_ready, 1)

            @block.vector
            def _(dve):
                dve.sem_inc(put, LAG)
                dve.wait_ge(w_loaded, 16 * len(loads))
                nc.vector.tensor_scalar(own[:, :, :], own_in[:, :, :], float(math.sin(math.pi / 8) * MUL ** -0.5), None, ALU.mult).then_inc(w_ready, 1)
                nc.vector.tensor_scalar(scale[:, :], k["isq"][:, :], float(math.cos(math.pi / 8) * (2 * MUL) ** -0.5), None, ALU.mult).then_inc(w_ready, 1)
                dve.wait_ge(w_ready, 2)
                dve.sem_inc(seen, 1)
                with dve.Fori(0, NG) as g:
                    def shrink(j):
                        b, back = buffer_of(j)
                        s = g * GN + j
                        dve.wait_ge(turned, s - back + 1 + LAG)
                        nc.vector.tensor_scalar(mid[:, b, :], flat(k["AGG2"][:, bass.ds(s, 1), :]), scale[:, bass.ds(s, 1)], None, ALU.mult).then_inc(mid_ready, 1)
                    shrink(0)
                    for j in range(GN):
                        b, back = buffer_of(j)
                        s = g * GN + j
                        if j + 1 < GN:
                            shrink(j + 1)
                        x = flat(k["X"][:, bass.ds(s, 1), :])
                        dve.wait_ge(made, s + 1)
                        nc.vector.scalar_tensor_tensor(x[:, 0:MUL], ps_o[b][:, 0:MUL], attr[:, bass.ds(s, 1)], x[:, 0:MUL], ALU.mult, ALU.add)
                        nc.vector.scalar_tensor_tensor(by_component(x), ps_o[b][:, MUL:D].rearrange("p (m u) -> p m u", m=3), attr[:, bass.ds(s, 1)],
                                                       by_component(x), ALU.mult, ALU.add).then_inc(put, 1)

            @block.scalar
            def _(act):
                with act.Fori(0, NG) as g:
                    for j in range(GN):
                        b, _ = buffer_of(j)
                        s = g * GN + j
                        act.wait_ge(turned, s + 1 + LAG)
                        nc.scalar.copy(both_T[:, b, 0:4, :].rearrange("p c n -> p (c n)"), ps_m[b][:, :])
                        nc.scalar.copy(both_T[:, b, 4:6, :].rearrange("p c n -> p (c n)"), ps_x[b][:, 0:2 * P]).then_inc(both_ready, 1)

            @block.tensor
            def _(pe):
                pe.sem_inc(turned, LAG)
                pe.wait_ge(w_ready, 2)
                with pe.Fori(0, NG) as g:
                    def turn(j):
                        b, _ = buffer_of(j)
                        pe.wait_ge(mid_ready, g * GN + j + 1)
                        pe.wait_ge(xp_ready, g * GN + j + 1)
                        for c in range(4):
                            nc.tensor.transpose(ps_m[b][:, c * P:(c + 1) * P], mid[:, b, c * P:(c + 1) * P], k["ident"][:, :])
                        for c in range(2):
                            ins = nc.tensor.transpose(ps_x[b][:, c * P:(c + 1) * P], xp[:, b, c * P:(c + 1) * P], k["ident"][:, :])
                        ins.then_inc(turned, 1)
                    turn(0)
                    for j in range(GN):
                        b, back = buffer_of(j)
                        s = g * GN + j
                        if j + 1 < GN:
                            turn(j + 1)
                        pe.wait_ge(both_ready, s + 1)
                        pe.wait_ge(put, s - back + 1 + LAG)
                        nc.tensor.matmul(ps_o[b][:, 0:D], k["zeros"][0:1, 0:P], k["zeros"][0:1, 0:D], start=True, stop=False)
                        for c in range(2):
                            nc.tensor.matmul(ps_o[b][:, c * P:(c + 1) * P], both_T[:, b, 4 + c, :], own[:, c, :], start=False, stop=False)
                        for c in range(4):
                            ins = nc.tensor.matmul(ps_o[b][:, c * MUL:(c + 1) * MUL], both_T[:, b, c, :], mid_w[:, min(c, 1), :], start=False, stop=(c == 3))
                        ins.then_inc(made, 1)


def last_norm(nc, k, out):
    with Phase(nc, "ln") as phase:
        sb, ps, sem = phase.sb, phase.ps, phase.sem
        stats, mean_var, rstd = sb("stats", [P, GN, 6]), sb("mean_var", [P, GN, 2]), sb("rstd", [P, GN])
        dve_step, seen, std_wanted, std_ready, normed, stored = (sem(n) for n in ("dve_step", "seen", "std_wanted", "std_ready", "normed", "stored"))
        STEPS = 4
        with nc.Block() as block:
            @block.vector
            def _(dve):
                with dve.Fori(0, NG) as g:
                    step = Count(dve, dve_step, g, STEPS)
                    statistics(nc, dve, step, [flat(k["X"][:, bass.ds(g * GN + j, 1), :]) for j in range(GN)], stats, mean_var,
                               (std_wanted, seen), std_ready, g, rstd)
                    for j in range(GN):
                        z = flat(k["X"][:, bass.ds(g * GN + j, 1), :])
                        ins = nc.vector.tensor_scalar(z, z, mean_var[:, j, 0:1], rstd[:, j:j + 1], ALU.subtract, ALU.mult)
                    step.then_wait(ins)
                    dve.sem_inc(normed, 1)
                    step.full()

            @block.scalar
            def _(act):
                with act.Fori(0, NG) as g:
                    act.wait_ge(std_wanted, g + 1)
                    nc.scalar.activation(rstd[:, :], rstd[:, :], ACT.Sqrt).then_inc(std_ready, 1)

            @block.sync
            def _(sp):
                with sp.Fori(0, NG - 1) as g:
                    sp.wait_ge(normed, g + 1)
                    sp.dma_start(out[bass.ds(g * GN * P, GN * P), :].rearrange("(t p) d -> p t d", p=P), k["X"][:, bass.ds(g * GN, GN), :]).then_inc(stored, 16)
                sp.wait_ge(normed, NG)
                sp.dma_start(out[(NT - GN) * P:(NT - 1) * P, :].rearrange("(t p) d -> p t d", p=P), k["X"][:, NT - GN:NT - 1, :]).then_inc(stored, 16)
                sp.dma_start(out[(NT - 1) * P:N, :], k["X"][0:NLAST, NT - 1, :]).then_inc(stored, 16)
                sp.wait_ge(stored, 16 * (NG + 1))


def kernel(**inputs):
    import numpy as np
    import concourse.bacc as bacc
    from concourse.bass_utils import run_bass_kernel_spmd as run

    def padded(name, fill=0):
        a = np.asarray(inputs[name])
        p = np.full((ET * P,) + a.shape[1:], fill, a.dtype)
        p[:E] = a
        return p

    def by_tile(a):
        return np.ascontiguousarray(np.moveaxis(a.reshape((ET, P) + a.shape[1:]), 1, 0))

    arrays = {
        "x": inputs["x"],
        "src": by_tile(padded("src")),
        "dst": by_tile(padded("dst", PAD_NODE)),
        "dst_rows": padded("dst", PAD_NODE).reshape(ET, P),
        "rel": by_tile(padded("edge_type_16")),
        "norm": by_tile(padded("edge_weight1")[:, 0]),
        "etype": by_tile(padded("edge_type_64")),
        "y": by_tile(padded("edge_attr_4")),
        "node_attr": np.concatenate([np.asarray(inputs["node_vec1"])[:, 0], np.zeros(NT * P - N, np.float32)]).reshape(NT, P).T,
        "ea10": padded("edge_attr_10").reshape(ET, P, NB).transpose(0, 2, 1),
        "ea256": padded("edge_attr_256").reshape(ET, P, 2, P).transpose(0, 3, 2, 1),
    }
    for short, name in (("w0", "L0_gnn_weight"), ("w_msg", "L1_gnn_W_msg"), ("b_msg", "L1_gnn_b_msg"), ("w_upd", "L1_gnn_W_upd"),
                        ("b_upd", "L1_gnn_b_upd"), ("q_emb", "L2_gnn_query_emb"), ("wq", "L2_gnn_Wq"), ("bq", "L2_gnn_bq"),
                        ("wk", "L2_gnn_Wk"), ("bk", "L2_gnn_bk"), ("wv", "L2_gnn_Wv"), ("bv", "L2_gnn_bv"), ("rel_w", "L2_gnn_rel_w"),
                        ("wo", "L2_gnn_Wo"), ("bo", "L2_gnn_bo"), ("gamma", "L2_gnn_gamma"), ("beta", "L2_gnn_beta"),
                        ("w_li0", "L3_gnn_W_li0"), ("w_li1", "L3_gnn_W_li1"), ("w_lm0", "L3_gnn_W_lm0"), ("w_lm1", "L3_gnn_W_lm1"),
                        ("w_mlp1", "L3_gnn_W_mlp1"), ("w_mlp2", "L3_gnn_W_mlp2"), ("w_lo0", "L3_gnn_W_lo0"), ("w_lo1", "L3_gnn_W_lo1")):
        arrays[short] = inputs[name]
    arrays = {n: np.ascontiguousarray(a) for n, a in arrays.items()}
    nc = bacc.Bacc("TRN2", target_bir_lowering=False, num_devices=1)
    args = {n: nc.dram_tensor(n, a.shape, mybir.dt.from_np(a.dtype), kind="ExternalInput").ap() for n, a in arrays.items()}
    for n, shape in (("rel_rows", (NT * P, R * D)), ("src_table", (NT * P, D)), ("key_table", (NT * P, D)),
                     ("value_table", (NT * P, D)), ("score_rows", (ET * H, P))):
        args[n] = nc.dram_tensor(n, shape, F32, kind="Internal").ap()
    args["out"] = nc.dram_tensor("out", (N, D), F32, kind="ExternalOutput").ap()
    gnn(nc, **args)
    return run(nc, [arrays], core_ids=[0]).results[0]["out"]
```
